# Optimizing a Trainium2 kernel written in Bass

```python
import numpy as np
import jax
import jax.numpy as jnp

def _softmax(x, axis=-1):
    return jax.nn.softmax(x, axis=axis)

def _gelu(x):
    return jax.nn.gelu(x, approximate=True)

def _silu(x):
    return jax.nn.silu(x)

def _sigmoid(x):
    return jax.nn.sigmoid(x)

def _layernorm(x, axis=-1, eps=1e-05):
    m = jnp.mean(x, axis=axis, keepdims=True)
    v = jnp.var(x, axis=axis, keepdims=True)
    return (x - m) / jnp.sqrt(v + eps)

def _scatter_add(tgt, idx, src, axis=0):
    return tgt.at[idx].add(src)

def _segment_sum(src, seg, n):
    return jax.ops.segment_sum(src, seg, n)
kernel_name = 'mk_gnn_resnorm_d2_gnn_r8_07e23e'

def setup_inputs(seed: int=0):
    np.random.seed(seed)
    _w = jnp.asarray

    def _rec_inputs():
        import jax
        import jax.numpy as jnp
        _gk = jax.random.key(seed)
        x = -0.000202 + 1 * jax.random.normal(jax.random.fold_in(_gk, 1), (6250, 128), jnp.float32)
        src = jax.random.randint(jax.random.fold_in(_gk, 2), (100000,), 0, 6250, jnp.int32)
        dst = jnp.minimum((6250 * jax.random.uniform(jax.random.fold_in(_gk, 3), (100000,)) ** 2.0).astype(jnp.int32), 49999)
        _o = jnp.argsort(dst, stable=True)
        src = src[_o]
        dst = dst[_o]
        edge_attr_16 = 0.00028786 + 0.999816 * jax.random.normal(jax.random.fold_in(_gk, 11), (100000, 16), jnp.float32)
        return (x, src, dst, edge_attr_16)
    x, src, dst, edge_attr_16 = _rec_inputs()

    def _L0_gnn_setup():
        import jax, jax.numpy as jnp
        import numpy as np
        N_NODES = 6250
        N_EDGES = 100000
        HIDDEN = 128
        N_LAYERS = 3

        def _sage_layer(x, src, dst, Wl_i, bl_i, Wr_i):
            msg = x[src]
            agg = jax.ops.segment_sum(msg, dst, num_segments=N_NODES)
            cnt = jax.ops.segment_sum(jnp.ones((src.shape[0],), x.dtype), dst, num_segments=N_NODES)
            mean = agg / jnp.clip(cnt, 1.0)[:, None]
            return mean @ Wl_i + bl_i + x @ Wr_i
        key = jax.random.key(seed)
        ks = jax.random.split(key, 6)
        x = jax.random.normal(ks[0], (N_NODES, HIDDEN), dtype=jnp.float32)
        edge_index = jax.random.randint(ks[1], (2, N_EDGES), 0, N_NODES, dtype=jnp.int64)
        scale = 1.0 / np.sqrt(HIDDEN)
        Wl = jax.random.normal(ks[2], (N_LAYERS, HIDDEN, HIDDEN), dtype=jnp.float32) * scale
        bl = jax.random.normal(ks[3], (N_LAYERS, HIDDEN), dtype=jnp.float32) * scale
        Wr = jax.random.normal(ks[4], (N_LAYERS, HIDDEN, HIDDEN), dtype=jnp.float32) * scale
        return {'x': x, 'edge_index': edge_index, 'Wl': Wl, 'bl': bl, 'Wr': Wr}
    _L0_gnn_all = _L0_gnn_setup()
    _L0_gnn_in = {k: v for k, v in _L0_gnn_all.items() if k in ('Wl', 'bl', 'Wr')}
    del _L0_gnn_all

    def _L1_gnn_setup():
        import jax, jax.numpy as jnp
        import numpy as np
        N, F, ED, E = (2500, 128, 16, 75000)
        EPS = 1e-05
        key = jax.random.key(seed)
        ks = jax.random.split(key, 8)
        x = jax.random.normal(ks[0], (N, F), dtype=jnp.float32)
        edge_index = jax.random.randint(ks[1], (2, E), 0, N, dtype=jnp.int64)
        edge_attr = jax.random.normal(ks[2], (E, ED), dtype=jnp.float32)
        zdim = 2 * F + ED
        sc = 1.0 / np.sqrt(zdim)
        Wf = jax.random.uniform(ks[3], (F, zdim), jnp.float32, -sc, sc)
        bf = jax.random.uniform(ks[4], (F,), jnp.float32, -sc, sc)
        Ws = jax.random.uniform(ks[5], (F, zdim), jnp.float32, -sc, sc)
        bs = jax.random.uniform(ks[6], (F,), jnp.float32, -sc, sc)
        bn_gamma = jnp.ones((F,), jnp.float32)
        bn_beta = jnp.zeros((F,), jnp.float32)
        ln_gamma = jnp.ones((F,), jnp.float32)
        ln_beta = jnp.zeros((F,), jnp.float32)
        return {'x': x, 'edge_index': edge_index, 'edge_attr': edge_attr, 'Wf': Wf, 'bf': bf, 'Ws': Ws, 'bs': bs, 'bn_gamma': bn_gamma, 'bn_beta': bn_beta, 'ln_gamma': ln_gamma, 'ln_beta': ln_beta}
    _L1_gnn_all = _L1_gnn_setup()
    _L1_gnn_in = {k: v for k, v in _L1_gnn_all.items() if k in ('Wf', 'bf', 'Ws', 'bs', 'bn_gamma', 'bn_beta', 'ln_gamma', 'ln_beta')}
    del _L1_gnn_all
    return {'x': x, 'src': src, 'dst': dst, 'edge_attr_16': edge_attr_16, 'L0_gnn_Wl': _L0_gnn_in['Wl'], 'L0_gnn_bl': _L0_gnn_in['bl'], 'L0_gnn_Wr': _L0_gnn_in['Wr'], 'L1_gnn_Wf': _L1_gnn_in['Wf'], 'L1_gnn_bf': _L1_gnn_in['bf'], 'L1_gnn_Ws': _L1_gnn_in['Ws'], 'L1_gnn_bs': _L1_gnn_in['bs'], 'L1_gnn_bn_gamma': _L1_gnn_in['bn_gamma'], 'L1_gnn_bn_beta': _L1_gnn_in['bn_beta'], 'L1_gnn_ln_gamma': _L1_gnn_in['ln_gamma'], 'L1_gnn_ln_beta': _L1_gnn_in['ln_beta']}

def reference(x, src, dst, edge_attr_16, L0_gnn_Wl, L0_gnn_bl, L0_gnn_Wr, L1_gnn_Wf, L1_gnn_bf, L1_gnn_Ws, L1_gnn_bs, L1_gnn_bn_gamma, L1_gnn_bn_beta, L1_gnn_ln_gamma, L1_gnn_ln_beta):
    import jax
    import jax.numpy as jnp

    def _L0_gnn_ref(x, edge_index, Wl, bl, Wr):
        import jax, jax.numpy as jnp
        import numpy as np
        N_NODES = 6250
        N_EDGES = 100000
        HIDDEN = 128
        N_LAYERS = 3

        def _sage_layer(x, src, dst, Wl_i, bl_i, Wr_i):
            msg = x[src]
            agg = jax.ops.segment_sum(msg, dst, num_segments=N_NODES)
            cnt = jax.ops.segment_sum(jnp.ones((src.shape[0],), x.dtype), dst, num_segments=N_NODES)
            mean = agg / jnp.clip(cnt, 1.0)[:, None]
            return mean @ Wl_i + bl_i + x @ Wr_i
        src, dst = (edge_index[0], edge_index[1])
        h = x
        for i in range(N_LAYERS):
            h = _sage_layer(h, src, dst, Wl[i], bl[i], Wr[i])
            if i < N_LAYERS - 1:
                h = jax.nn.relu(h)
        return h

    def _L1_gnn_ref(x, edge_index, edge_attr, Wf, bf, Ws, bs, bn_gamma, bn_beta, ln_gamma, ln_beta):
        import jax, jax.numpy as jnp
        import numpy as np
        N, F, ED, E = (2500, 128, 16, 75000)
        EPS = 1e-05
        n = x.shape[0]
        src, dst = (edge_index[0], edge_index[1])
        z = jnp.concatenate([x[dst], x[src], edge_attr], axis=-1)
        msg = jax.nn.sigmoid(z @ Wf.T + bf) * jax.nn.softplus(z @ Ws.T + bs)
        agg = jax.ops.segment_sum(msg, dst, num_segments=n)
        mu_b = agg.mean(axis=0)
        var_b = agg.var(axis=0)
        agg = (agg - mu_b) * jax.lax.rsqrt(var_b + EPS) * bn_gamma + bn_beta
        h = agg + x
        mu = h.mean(axis=-1, keepdims=True)
        var = h.var(axis=-1, keepdims=True)
        h = (h - mu) * jax.lax.rsqrt(var + EPS) * ln_gamma + ln_beta
        h = jax.nn.relu(h)
        return h + x
    edge_index = jnp.stack([src, dst])
    x = _layernorm(x + _L0_gnn_ref(x, edge_index, L0_gnn_Wl, L0_gnn_bl, L0_gnn_Wr), axis=-1)
    x = _layernorm(x + _L1_gnn_ref(x, edge_index, edge_attr_16, L1_gnn_Wf, L1_gnn_bf, L1_gnn_Ws, L1_gnn_bs, L1_gnn_bn_gamma, L1_gnn_bn_beta, L1_gnn_ln_gamma, L1_gnn_ln_beta), axis=-1)
    return x

_drawn_inputs = setup_inputs


def setup_inputs(seed=0):
    import zlib

    import numpy as np

    out = dict(_drawn_inputs(seed))
    spreads = {'L1_gnn_bn_gamma': (1.0, 0.535),
     'L1_gnn_bn_beta': (0.0, 0.275),
     'L1_gnn_ln_gamma': (1.0, 0.2),
     'L1_gnn_ln_beta': (0.0, 0.318)}
    factors = {'edge_attr_16': 8.0, 'L1_gnn_bf': 64.0, 'L1_gnn_bs': 64.0}
    for name, (base, spread) in spreads.items():
        noise = np.random.default_rng([zlib.crc32(name.encode()), seed]).standard_normal(out[name].shape)
        drawn = base * np.exp(spread * noise) if base else spread * noise
        out[name] = jnp.asarray(drawn.astype(out[name].dtype))
    for name, factor in factors.items():
        out[name] = (out[name] * factor).astype(out[name].dtype)
    return out
```

```python
import concourse.bass as bass
from concourse import mybir
from concourse.alu_op_type import AluOpType as ALU
from contextlib import ExitStack

P = 128
N = 6250
E = 100000
F = 128
ED = 16
NW = -(-N // P)
NP = NW * P
NT = -(-E // P)
EP = NT * P
G = 4
UB = 16
GB = UB // G
NS = -(-(NT + NW - 1) // UB) * UB
NG = NS // G
NC = -(-NS // P)
CW = 7
NCH = NW // CW
FA = F + 1
PAD = 1 << 20
EPS = 1e-5
assert NW == CW * NCH and EP == P * NT


def build_gnn(nc, x, xT, src, dst, ea, eaT, w0, bl, blT, w1, we, b1, bn, out):
    f32, i32, bf16 = mybir.dt.float32, mybir.dt.int32, mybir.dt.bfloat16
    ACT = mybir.ActivationFunctionType
    X = mybir.AxisListType.X
    ctx = ExitStack()
    with ctx:
        def sb(name, shape, dt=f32):
            return ctx.enter_context(nc.sbuf_tensor(name, shape, dt))

        def sem(name):
            return ctx.enter_context(nc.semaphore(name))

        def dram(name, shape, dt=f32):
            return nc.dram_tensor(name, shape, dt).ap()

        def every_partition(row, n):
            return bass.AP(row.tensor, row.offset, [[0, P], [1, n]])

        y_dram = dram("y_dram", (NP, F))
        q_dram = dram("q_dram", (NP, 2 * F))
        dst_sorted = dram("dst_sorted", (NT, P), i32)
        src_sorted = dram("src_sorted", (NT, P), i32)
        eaT_sorted = dram("eaT_sorted", (ED, EP))
        regs_dram = dram("regs_dram", (3, NC * P), i32)
        fb_dst = dram("fb_dst", (EP, 1), i32)
        fb_src = dram("fb_src", (EP, 1), i32)
        fb_ea = dram("fb_ea", (EP, ED))

        x_sb = sb("x_sb", [P, NW * F])
        acc = sb("acc", [P, NW * FA])
        pq = sb("pq", [P, NW * 2 * F])
        r_off = NW * F
        res = pq[:, r_off:2 * r_off]
        dlo = sb("dlo", [P, NC * P])
        srcs = sb("srcs", [P, NC * P], i32)
        regs = sb("regs", [1, 3 * NC * P], i32)
        xT_sb = acc[:, 0:NW * F]
        zero = sb("zero", [P, 1])
        iota = sb("iota", [P, P])
        ident = sb("ident", [P, P])
        ones = sb("ones", [P, P])
        mask = sb("mask", [P, P])
        w0_sb = sb("w0_sb", [P, 3, 2 * F])
        w1_sb = sb("w1_sb", [P, 4 * F])
        we_sb = sb("we_sb", [ED, 2 * F])
        blT_sb = sb("blT_sb", [P, 3])
        bl2 = sb("bl2", [P, F])
        b1_sb = sb("b1_sb", [P, 2 * F])
        bn_sb = sb("bn_sb", [P, 4, F])
        inv = sb("inv", [P, NW])
        cnt = sb("cnt", [P, NW])

        gath = sb("gath", [P, UB, 2 * F])
        msg = gath[:, :, 0:FA]
        qg = gath[:, :, :].rearrange("p (g t) f -> p g t f", t=G)
        idx = sb("idx", [P, UB], i32)

        work = sb("work", [P, 9728])
        hr = work[:, 0:896].rearrange("p (u f) -> p u f", f=F)
        hT = work[:, 896:1792].rearrange("p (u f) -> p u f", f=F)
        Y_STAGE, Q_STAGE = 1792, 1792
        oh4 = work[:, 3584:4096].rearrange("p (u f) -> p u f", f=P)
        tmp = work[:, 3584:4480].rearrange("p (u f) -> p u f", f=F)
        tmp2 = work[:, 4480:5376].rearrange("p (u f) -> p u f", f=F)
        oh = work[:, 0:2048].rearrange("p (g t f) -> p g t f", g=GB, t=G)
        ohT = work[:, 2048:3072].rearrange("p (g t f) -> p g t f", g=2, t=G)
        pre = work[:, 3072:5120].rearrange("p (g t f) -> p g t f", g=2, t=G)
        lg = work[:, 5120:7168].rearrange("p (g t f) -> p g t f", g=2, t=G)
        sg = work[:, 7168:7680].rearrange("p (t f) -> p t f", t=G)
        sp_ = work[:, 7680:8192].rearrange("p (t f) -> p t f", t=G)
        mm = work[:, 8192:9216].rearrange("p (g t f) -> p g t f", g=2, t=G)
        ea_sb = sb("ea_sb", [ED, UB, P])
        mean = sb("mean", [P, F])
        bscale = sb("bscale", [P, F])
        small = sb("small", [P, 4, F])
        st6 = sb("st6", [P, CW, 6])
        mv = sb("mv", [P, CW, 2])
        ve = sb("ve", [P, CW])
        rs = sb("rs", [P, CW])
        rt = sb("rt", [P, CW])
        cen = pq[:, 0:NW * F]

        at = [0]

        def part(n, dt=f32):
            v = pq[:, at[0]:at[0] + n]
            at[0] += n
            return v if dt == f32 else v.bitcast(dt)

        d_nat = part(NT + 1, i32)
        d_f = part(NT + 1)
        junk = part(NT)
        d_win = work[:, 5376:5376 + NT // 2].bitcast(bf16)
        d_rows = part(NC * P, i32)
        s_rows = part(NC * P, i32)
        d_rowsf = part(NC * P)
        s_rowsf = part(NC * P)
        assert at[0] <= r_off
        NB = NW + 1
        sch = sb("sch", [P, 20, 52])
        schi = sb("schi", [P, 4, 52], i32)
        kcol = sb("kcol", [P, NC])
        tki = sb("tki", [P, NC], i32)
        tabf = sb("tabf", [P, 3, NC])
        tabi = sb("tabi", [P, 3, NC], i32)
        flag = sb("flag", [P, 1], i32)
        tri = sb("tri", [P, P])
        fd = sb("fd", [P, 1], i32)
        fs = sb("fs", [P, 1], i32)
        fe = sb("fe", [P, ED])
        fhi = sb("fhi", [P, 1], i32)
        fpos = sb("fpos", [P, 1], i32)
        fcol = sb("fcol", [P, 4])
        f_oh = sb("f_oh", [P, 52])
        f_tmp = sb("f_tmp", [P, 52])
        f_base = sb("f_base", [P, 52])

        ps = ctx.enter_context(nc.psum_tensor("ps", [P, 8, 512], f32))
        ps_prod = ps[:, 0:4, :].rearrange("p b (h f) -> p (b h) f", h=2)
        ps_tr = ps[:, 4:8, :].rearrange("p b (h f) -> p (b h) f", h=4)
        ps_pre = ps[:, 0:4, :].rearrange("p (g b) (h f) -> p g (b h) f", g=2, h=2)
        ps_ohT = ps[:, 4:6, :].rearrange("p g (t f) -> p g t f", t=G)
        ps_agg = ps[:, 6:8, :].rearrange("p g (t f) -> p g t f", t=G)

        names = """const loads dnat w0_in xT_first xT_rest y_written products dve cnt S
            tki tab tab_back idx_given idx_sorted ea_sorted rows rowsf rows_tr dlo_ready srcs_ready
            fl f_onehot f_rank f_pos f_scattered f_done
            idx_ready onehots tiles_added tiles_summed h_ready h_transposed h_copied
            prod_act prod_dve z_var z_rs x1_ready x1_tr x1_copied x1_prod p_done q_staged q_written x_kept acc_clear
            qi oh1 oh_tr oh_copied pre_ready added absd expd logd diffd sigd spd msgd agg
            agg_added bn_sum bn_sq sq_ready sq_used cen_ready bv_var bv_rs
            passed y_free q_free o_free f_free t_scaled t_used t_var t_rs o_ready o_written ones_col"""
        s = {n: sem("s_" + n) for n in names.split()}
        s_msg = [sem(f"s_msg{u}") for u in range(UB)]
        s_qg = [sem(f"s_qg{g}") for g in range(GB)]
        s_ea = [sem(f"s_ea{g}") for g in range(GB)]
        LOADS = 8
        FROM_ONE = ("products", "t_used", "prod_act", "prod_dve", "h_copied", "x1_copied", "x1_prod", "h_transposed", "x1_tr", "x_kept", "o_ready", "q_free", "spd", "msgd", "diffd", "y_free", "q_free", "o_free", "f_free")

        block = ctx.enter_context(nc.Block())

        def alone(engine):
            engine.sem_inc(s["passed"], 1)

        PAIRS = [(0, 1), (2, 3), (4, 5), (6,)]
        QUADS = [(0, 1, 2, 3), (4, 5, 6)]
        XT_PARTS = [(0, 2), (2, NCH)]
        P_BANKS = (0, 1, 6, 7)

        def y_staged(slot, w=0, n=CW):
            return work[:, bass.ds(slot * (CW * F) + (Y_STAGE + w * F), n * F)].rearrange("p (u f) -> p u f", f=F)

        def q_staged(slot, w=0, n=CW):
            return work[:, bass.ds(slot * (CW * 2 * F) + (Q_STAGE + w * 2 * F), n * 2 * F)]\
                .rearrange("p (u f) -> p u f", f=2 * F)

        def chunk(t, it, n):
            return t[:, bass.ds(it * (CW * n), CW * n)].rearrange("p (u f) -> p u f", f=n)

        @block.sync
        def _(sp):
            for name, slots in (("tiles_summed", UB), ("tiles_added", 4), ("p_done", 4), ("q_staged", 2), ("pre_ready", GB),
                                ("added", GB), ("oh_copied", 2), ("agg", GB), ("agg_added", 2 * G)):
                sp.sem_inc(s[name], slots)
            for name in FROM_ONE:
                sp.sem_inc(s[name], 1)
            d_flat = bass.AP(dst.tensor, dst.offset, [[NT, P], [1, NT + 1]])
            sp.dma_start(d_nat, d_flat).then_inc(s["dnat"], 16)
            sp.dma_start(w0_sb[:, :, :], w0.rearrange("l k n -> k l n")).then_inc(s["w0_in"], 16)
            for part_, (c0, c1) in zip(("xT_first", "xT_rest"), XT_PARTS):
                sp.dma_start(xT_sb[:, c0 * CW * P:c1 * CW * P], xT[:, c0 * CW * P:c1 * CW * P]).then_inc(s[part_], 16)
            d2 = dst[0:EP].rearrange("(t e) -> t e", e=P)
            s2 = src[0:EP].rearrange("(t e) -> t e", e=P)
            sp.dma_start(dst_sorted, d2).then_inc(s["idx_given"], 16)
            sp.dma_start(src_sorted, s2).then_inc(s["idx_given"], 16)
            with sp.Fori(0, NCH) as it:
                sp.wait_ge(s["prod_act"], (it + 1) * 2 + 1)
                sp.dma_start(y_dram[bass.ds(it * (CW * P), CW * P), :].rearrange("(u p) f -> p u f", p=P),
                             y_staged(it % 2)).then_inc(s["y_written"], 16)
                sp.wait_ge(s["y_written"], (it + 1) * 16)
                sp.sem_inc(s["y_free"], 1)
            sp.wait_ge(s["tki"], 1)
            unsorted = sp.value_load(flag[0:1, 0:1], min_val=0, max_val=P)
            with sp.If(unsorted > 0):
                with sp.Fori(0, NT) as t:
                    sp.wait_ge(s["f_free"], t + 1)
                    with nc.allow_non_contiguous_dma(reason="a column of indices"):
                        sp.dma_start(fd[:, :], dst[bass.ds(t * P, P)].rearrange("(e o) -> e o", o=1)).then_inc(s["fl"], 16)
                        sp.dma_start(fs[:, :], src[bass.ds(t * P, P)].rearrange("(e o) -> e o", o=1)).then_inc(s["fl"], 16)
                    sp.dma_start(fe[:, :], ea[bass.ds(t * P, P), :]).then_inc(s["fl"], 16)
                sp.wait_ge(s["f_scattered"], NT * 48)
                sp.wait_ge(s["idx_given"], 32)
                sp.dma_start(dst_sorted, fb_dst.rearrange("(t e) o -> t (e o)", e=P)).then_inc(s["idx_sorted"], 16)
                sp.dma_start(src_sorted, fb_src.rearrange("(t e) o -> t (e o)", e=P)).then_inc(s["idx_sorted"], 16)
                with nc.allow_non_contiguous_dma(reason="edge attributes transposed"):
                    for h in range(2):
                        sp.dma_start(eaT_sorted[:, h * EP // 2:(h + 1) * EP // 2],
                                     fb_ea[h * EP // 2:(h + 1) * EP // 2, :].rearrange("e k -> k e"))\
                            .then_inc(s["ea_sorted"], 16)
            sp.wait_ge(s["tab"], 1)
            with nc.allow_non_contiguous_dma(reason="the schedule, transposed"):
                for r in range(3):
                    sp.dma_start(regs_dram[r, :].rearrange("(c p) -> p c", p=P), tabi[:, r, :]).then_inc(s["tab_back"], 16)
            sp.wait_ge(s["tab_back"], 48)
            sp.dma_start(regs[:, :], regs_dram.rearrange("(o r) k -> o (r k)", o=1)).then_inc(s["tab_back"], 16)
            with sp.If(unsorted < 1):
                sp.wait_ge(s["rows"], 2 * NC * 16)
                for h in range(2):
                    sp.dma_start(eaT_sorted[:, h * EP // 2:(h + 1) * EP // 2],
                                 eaT[:, h * EP // 2:(h + 1) * EP // 2]).then_inc(s["ea_sorted"], 16)
            with sp.Fori(0, 2) as layer:
                with sp.Fori(0, NCH) as it:
                    sp.wait_ge(s["prod_act"], ((layer + 1) * NCH + it + 1) * 2 + 1)
                    sp.wait_ge(s["prod_dve"], ((layer + 1) * NCH + it + 1) * 2 + 1)
                    sp.dma_start(y_dram[bass.ds(it * (CW * P), CW * P), :].rearrange("(u p) f -> p u f", p=P),
                                 y_staged(it % 2)).then_inc(s["y_written"], 16)
                    sp.wait_ge(s["y_written"], ((layer + 1) * NCH + it + 1) * 16)
                    sp.sem_inc(s["y_free"], 1)
            with sp.Fori(0, NCH) as it:
                sp.wait_ge(s["q_staged"], (it + 1) * 4 + 2)
                sp.dma_start(q_dram[bass.ds(it * (CW * P), CW * P), :].rearrange("(u p) f -> p u f", p=P),
                             q_staged(it % 2)).then_inc(s["q_written"], 16)
                sp.wait_ge(s["q_written"], (it + 1) * 16)
                sp.sem_inc(s["q_free"], 1)
            sp.wait_ge(s["ea_sorted"], 32)
            tile_regs = [sp.alloc_register(f"sp_tile{u}") for u in range(UB)]
            with sp.Fori(0, NG // GB) as m:
                sp.reg_load(tile_regs, regs[0:1, bass.ds(m * UB + 2 * NC * P, UB)])
                cols = [sp.snap(r, min_val=0, max_val=EP - P) for r in tile_regs]
                for g in range(GB):
                    sp.wait_ge(s["pre_ready"], m * GB + g + 1)
                    alone(sp)
                    for t in range(G):
                        sp.dma_start(ea_sb[:, g * G + t, :], eaT_sorted[:, bass.ds(cols[g * G + t], P)])\
                            .then_inc(s_ea[g], 16)
            full = N // P // CW * CW
            with sp.Fori(0, NCH - 1) as it:
                sp.wait_ge(s["o_ready"], it + 1 + 1)
                sp.dma_start(out[bass.ds(it * (CW * P), CW * P), :].rearrange("(u p) f -> p u f", p=P), hr)\
                    .then_inc(s["o_written"], 16)
                sp.wait_ge(s["o_written"], (it + 1) * 16)
                sp.sem_inc(s["o_free"], 1)
            sp.wait_ge(s["o_ready"], NCH + 1)
            last = (NCH - 1) * CW * P
            nfull = (N - last) // P
            sp.dma_start(out[last:last + nfull * P, :].rearrange("(u p) f -> p u f", p=P), hr[:, 0:nfull, :])\
                .then_inc(s["o_written"], 16)
            rest = N - last - nfull * P
            sp.dma_start(out[last + nfull * P:N, :], hr[0:rest, nfull, :]).then_inc(s["o_written"], 16)
            sp.wait_ge(s["o_written"], 16 * (NCH + 1))

        @block.gpsimd
        def _(pool):
            gp = nc.gpsimd
            gp.memset(ones[:, :], 1.0).then_inc(s["const"], 1)
            gp.memset(ident[:, :], 0.0).then_inc(s["const"], 1)
            gp.memset(tri[:, :], 1.0).then_inc(s["const"], 1)
            gp.memset(mask[:, :], 1.0).then_inc(s["const"], 1)
            gp.memset(gath[:, :, F:FA], 1.0).then_inc(s["ones_col"], 1)
            gp.iota(iota[:, :], pattern=[[1, P]], base=0, channel_multiplier=0,
                    allow_small_or_imprecise_dtypes=True).then_inc(s["const"], 1)
            gp.iota(kcol[:, :], pattern=[[P, NC]], base=0, channel_multiplier=1,
                    allow_small_or_imprecise_dtypes=True).then_inc(s["const"], 1)
            pool.wait_ge(s["const"], 6)
            gp.affine_select(out=ident[:, :], in_=ident[:, :], compare_op=ALU.not_equal, fill=1.0, base=0,
                             pattern=[[-1, P]], channel_multiplier=1).then_inc(s["const"], 1)
            gp.affine_select(out=tri[:, :], in_=tri[:, :], compare_op=ALU.is_gt, fill=0.0, base=0,
                             pattern=[[1, P]], channel_multiplier=-1).then_inc(s["const"], 1)
            gp.affine_select(out=mask[:, :], in_=mask[:, :], compare_op=ALU.is_gt, fill=0.0,
                             base=N - (NW - 1) * P, pattern=[[0, P]], channel_multiplier=-1).then_inc(s["const"], 1)
            pool.wait_ge(s["tki"], 1)
            unsorted = pool.value_load(flag[0:1, 0:1], min_val=0, max_val=P)
            with pool.If(unsorted > 0):
                with pool.Fori(0, NT) as t:
                    pool.wait_ge(s["f_pos"], t + 1)
                    alone(pool)
                    off = bass.IndirectOffsetOnAxis(ap=fpos[:, 0:1], axis=0)
                    pool.indirect_dma_start(fb_dst, off, fd[:, :], None).then_inc(s["f_scattered"], 16)
                    pool.indirect_dma_start(fb_src, off, fs[:, :], None).then_inc(s["f_scattered"], 16)
                    pool.indirect_dma_start(fb_ea, off, fe[:, :], None).then_inc(s["f_scattered"], 16)
                    pool.wait_ge(s["f_scattered"], (t + 1) * 48)
                    pool.sem_inc(s["f_free"], 1)
                pool.wait_ge(s["idx_sorted"], 32)
            pool.wait_ge(s["idx_given"], 32)
            for c in range(NC):
                off = bass.IndirectOffsetOnAxis(ap=tki[:, c:c + 1], axis=0)
                pool.indirect_dma_start(d_rows[:, c * P:(c + 1) * P], None, dst_sorted, off).then_inc(s["rows"], 16)
                pool.indirect_dma_start(s_rows[:, c * P:(c + 1) * P], None, src_sorted, off).then_inc(s["rows"], 16)

            def sage_gathers(layer):
                pool.wait_ge(s["y_written"], (layer + 1) * (NCH * 16))
                alone(pool)
                with pool.Fori(0, NS // UB) as it:
                    for half in range(2):
                        pool.wait_ge(s["idx_ready"], layer * (2 * NS // UB) + it * 2 + half + 1)
                        alone(pool)
                        for u in range(half * UB // 2, (half + 1) * UB // 2):
                            pool.indirect_dma_start(
                                msg[:, u, 0:F], None, y_dram,
                                bass.IndirectOffsetOnAxis(ap=idx[:, u:u + 1], axis=0)).then_inc(s_msg[u], 16)

            with pool.Fori(0, 2) as layer:
                sage_gathers(layer)
            sage_gathers(2)
            with pool.Fori(0, NCH) as it:
                pool.wait_ge(s["x1_ready"], it + 1)
                gp.tensor_copy(x_sb[:, bass.ds(it * (CW * F), CW * F)], work[:, 0:896]).then_inc(s["x_kept"], 1)
            pool.wait_ge(s["q_written"], NCH * 16)
            with pool.Fori(0, NG // GB) as m:
                for g in range(GB):
                    pool.wait_ge(s["qi"], m * GB + g + 1)
                    alone(pool)
                    for t in range(G):
                        pool.indirect_dma_start(
                            qg[:, g, t, :], None, q_dram,
                            bass.IndirectOffsetOnAxis(ap=idx[:, g * G + t:g * G + t + 1], axis=0))\
                            .then_inc(s_qg[g], 16)
            pool.wait_ge(s["loads"], LOADS * 16)
            pool.wait_ge(s["bv_rs"], 3)
            with pool.Fori(0, NCH) as it:
                pool.wait_ge(s["t_used"], it + 1)
                gp.tensor_tensor(tmp, chunk(cen, it, F), bscale[:, :].unsqueeze(1).to_broadcast([P, CW, F]), ALU.mult)\
                    .then_inc(s["t_scaled"], 1)
                pool.wait_ge(s["t_scaled"], it * 2 + 1)
                gp.tensor_tensor(tmp, tmp, bn_sb[:, 1, :].unsqueeze(1).to_broadcast([P, CW, F]), ALU.add)\
                    .then_inc(s["t_scaled"], 1)

        @block.tensor
        def _(pe):
            te = nc.tensor
            pe.wait_ge(s["w0_in"], 16)

            for it in range(NCH):
                pe.wait_ge(s["xT_first" if it < XT_PARTS[0][1] else "xT_rest"], 16)
                pe.wait_ge(s["prod_act"], it * 2 + 1)
                pe.wait_ge(s["prod_dve"], it * 2 + 1)
                for b, wins in enumerate(PAIRS):
                    for u in wins:
                        w = it * CW + u
                        last = te.matmul(ps_prod[:, u, :], lhsT=xT_sb[:, w * P:(w + 1) * P], rhs=w0_sb[:, 0, :],
                                         start=True, stop=True)
                    last.then_inc(s["products"], 1)
                if it == NCH // 2:
                    pe.wait_ge(s["const"], 9)
                    pe.wait_ge(s["cnt"], 1)
                    te.matmul(ps[:, 6, 0:NB + 1], lhsT=ones[:, :], rhs=sch[:, 0, 0:NB + 1], start=True, stop=True)\
                        .then_inc(s["S"], 1)
            pe.wait_ge(s["loads"], LOADS * 16)
            pe.wait_ge(s["tki"], 1)
            unsorted = pe.value_load(flag[0:1, 0:1], min_val=0, max_val=P)
            with pe.If(unsorted > 0):
                with pe.Fori(0, NT) as t:
                    pe.wait_ge(s["f_onehot"], t + 1)
                    te.matmul(ps[:, 6, 0:NB], lhsT=tri[:, :], rhs=f_oh[:, 0:NB], start=True, stop=True)
                    te.matmul(ps[:, 7, 0:NB], lhsT=ones[:, :], rhs=f_oh[:, 0:NB], start=True, stop=True)\
                        .then_inc(s["f_rank"], 1)
            pe.wait_ge(s["rowsf"], 1)
            for c in range(2 * NC):
                rows, slot = (d_rowsf, c) if c < NC else (s_rowsf, c - NC + 8)
                last = te.transpose(ps_tr[:, slot, :], rows[:, c % NC * P:(c % NC + 1) * P], ident[:, :])
            last.then_inc(s["rows_tr"], 1)
            pe.wait_ge(s["ones_col"], 1)

            def sage_sums(layer):
                with pe.Fori(0, NS // UB) as it:
                    for u in range(UB):
                        step = layer * NS + it * UB + u
                        pe.wait_ge(s_msg[u], layer * (NS // UB * 16) + (it + 1) * 16)
                        pe.wait_ge(s["onehots"], step + 1)
                        pe.wait_ge(s["tiles_added"], step + 1)
                        te.matmul(ps[:, u % 4, 0:FA], lhsT=oh4[:, u % 4, :], rhs=msg[:, u, :],
                                  start=True, stop=True).then_inc(s["tiles_summed"], 1)

            def sage_layer(layer):
                sage_sums(layer)
                pe.wait_ge(s["tiles_added"], (layer + 1) * NS + 4)
                alone(pe)
                with pe.Fori(0, NCH) as it:
                    c = layer * NCH + it
                    for k, wins in enumerate(QUADS):
                        pe.wait_ge(s["h_ready"], c * CW + wins[-1] + 1)
                        pe.wait_ge(s["h_copied"], c * 2 + 1)
                        for u in wins:
                            last = te.transpose(ps_tr[:, u, :], hr[:, u, :], ident[:, :])
                        last.then_inc(s["h_transposed"], 1)
                    for b, wins in enumerate(PAIRS):
                        pe.wait_ge(s["h_copied"], c * 2 + b // 2 + 1 + 1)
                        pe.wait_ge(s["prod_dve"] if b % 2 else s["prod_act"], (c + NCH) * 2 + 1)
                        for u in wins:
                            last = te.matmul(ps_prod[:, u, :], lhsT=hT[:, u, :],
                                             rhs=w0_sb[:, bass.ds(layer + 1, 1), :].rearrange("p a n -> p (a n)"),
                                             start=True, stop=True)
                        last.then_inc(s["products"], 1)

            with pe.Fori(0, 2) as layer:
                sage_layer(layer)
            sage_sums(2)
            pe.wait_ge(s["tiles_added"], 3 * NS + 4)
            with pe.Fori(0, NCH) as it:
                pe.wait_ge(s["x1_ready"], it + 1)
                pe.wait_ge(s["x1_copied"], it * 2 + 1)
                for wins in QUADS:
                    for u in wins:
                        last = te.transpose(ps_tr[:, u, :], hr[:, u, :], ident[:, :])
                    last.then_inc(s["x1_tr"], 1)
                for b, wins in enumerate(PAIRS):
                    pe.wait_ge(s["x1_copied"], it * 2 + b // 2 + 1 + 1)
                    pe.wait_ge(s["p_done"], it * 4 + b + 1)
                    pe.wait_ge(s["q_staged"], it * 4 + b + 1)
                    for h in range(2):
                        for u in wins:
                            last = te.matmul(ps[:, 2 + b % 2 if h else P_BANKS[b], u % 2 * 2 * F:(u % 2 + 1) * 2 * F],
                                             lhsT=hT[:, u, :],
                                             rhs=w1_sb[:, h * 2 * F:(h + 1) * 2 * F], start=True, stop=True)
                    last.then_inc(s["x1_prod"], 1)

            pe.wait_ge(s["p_done"], NCH * 4 + 4)
            pe.wait_ge(s["q_staged"], NCH * 4 + 2)
            w_regs = [pe.alloc_register(f"pe_w{u}") for u in range(UB)]

            def load_windows(first):
                pe.reg_load(w_regs, regs[0:1, bass.ds(first + NC * P, UB)])
                return [pe.snap(r, min_val=0, max_val=(NW - 1) * 2 * F) for r in w_regs]

            def ok(g):
                return not isinstance(g, int) or 0 <= g < NG

            def conv_step(j, slot, m, wins, shift):
                g = j - 1
                if ok(g):
                    pe.wait_ge(s["oh_copied"], g + 3)
                    pe.wait_ge(s_ea[(slot - 1) % GB], ((g // GB if isinstance(g, int) else m - (1 if slot == 0 else 0)) + 1) * 64)
                    pe.wait_ge(s["added"], g + 3)
                    for t in range(G):
                        o = ps_pre[:, (slot - 1) % 2, t, :]
                        te.matmul(o, lhsT=ohT[:, (slot - 1) % 2, t, :],
                                  rhs=pq[:, bass.ds(wins[(slot - shift) * G + t], 2 * F)],
                                  start=True, stop=False)
                        last = te.matmul(o, lhsT=ea_sb[:, (slot - 1) % GB * G + t, :], rhs=we_sb[:, :],
                                         start=False, stop=True)
                    last.then_inc(s["pre_ready"], 1)
                if ok(j):
                    pe.wait_ge(s["oh1"], j + 1)
                    pe.wait_ge(s["oh_copied"], j + 1)
                    for t in range(G):
                        last = te.transpose(ps_ohT[:, slot % 2, t, :], oh[:, slot, t, :], ident[:, :])
                    last.then_inc(s["oh_tr"], 1)
                g = j - 3
                if ok(g):
                    pe.wait_ge(s["msgd"], g + 1 + 1)
                    pe.wait_ge(s["agg_added"], g * G + G)
                    for t in range(G):
                        last = te.matmul(ps_agg[:, (slot - 3) % 2, t, :], lhsT=oh[:, (slot - 3) % GB, t, :],
                                         rhs=mm[:, (slot - 3) % 2, t, :], start=True, stop=True)
                    last.then_inc(s["agg"], 1)

            wins = load_windows(0)
            for j in range(GB):
                conv_step(j, j, 0, wins, 1)
            with pe.Fori(1, NG // GB) as m:
                wins = load_windows(m * UB - G)
                for g in range(GB):
                    conv_step(m * GB + g, g, m, wins, 0)
            wins = load_windows(NS - G)
            for j in range(NG, NG + GB):
                conv_step(j, j % GB, NG // GB, wins, 0)
            pe.wait_ge(s["agg_added"], NS + 8)
            a3 = acc[:, :].rearrange("p (w f) -> p w f", f=FA)
            for w in range(0, NW, 4):
                n = min(4, NW - w)
                last = te.matmul(ps[:, 0, 0:n * F], lhsT=ones[:, :], rhs=a3[:, w:w + n, 0:F],
                                 start=w == 0, stop=w + n == NW)
            last.then_inc(s["bn_sum"], 1)
            for i, w in enumerate(range(0, NW, 4)):
                n = min(4, NW - w)
                pe.wait_ge(s["sq_ready"], i + 1)
                te.matmul(ps[:, 1, 0:n * F], lhsT=mask[:, :] if w + n == NW else ones[:, :],
                          rhs=work[:, 5376 + i % 2 * 512:5376 + i % 2 * 512 + n * F],
                          start=w == 0, stop=w + n == NW).then_inc(s["sq_used"], 1)

        @block.scalar
        def _(act):
            sc = nc.scalar
            act.dma_start(bl2[:, :], every_partition(bl[2, :], F)).then_inc(s["loads"], 16)
            act.dma_start(b1_sb[:, :], every_partition(b1, 2 * F)).then_inc(s["loads"], 16)
            act.dma_start(bn_sb[:, :, :].rearrange("p a f -> p (a f)"), every_partition(bn, 4 * F)).then_inc(s["loads"], 16)
            act.dma_start(blT_sb[:, :], blT).then_inc(s["loads"], 16)
            act.dma_start(w1_sb[:, :], w1).then_inc(s["loads"], 16)
            act.dma_start(we_sb[:, :], we).then_inc(s["loads"], 16)
            half = NW // 2 * P
            xv = x.rearrange("(w p) f -> p w f", p=P)
            xs = x_sb[:, :].rearrange("p (w f) -> p w f", f=F)
            act.dma_start(xs[:, 0:NW // 2, :], xv[:, 0:NW // 2, :]).then_inc(s["loads"], 16)
            act.dma_start(xs[:, NW // 2:NW, :], xv[:, NW // 2:NW, :]).then_inc(s["loads"], 16)
            def first_products(it):
                act.wait_ge(s["products"], (it + 1) * 4 + 1)
                sc.copy(y_staged(it % 2), ps_prod[:, 0:CW, 0:F]).then_inc(s["prod_act"], 2)
                sc.copy(chunk(res, it, F), ps_prod[:, 0:CW, F:2 * F]).then_inc(s["prod_dve"], 2)

            first_products(0)
            with act.Fori(1, NCH) as it:
                act.wait_ge(s["y_free"], it)
                first_products(it)
            act.wait_ge(s["rows_tr"], 1)
            act.wait_ge(s["loads"], LOADS * 16)
            sc.copy(dlo[:, :], ps_tr[:, 0:NC, :].rearrange("p c e -> p (c e)")).then_inc(s["dlo_ready"], 1)
            act.wait_ge(s["srcs_ready"], 1)

            def sage_indices(layer):
                with act.Fori(0, NS // UB) as it:
                    for half in range(2):
                        at_ = it * UB + half * (UB // 2)
                        act.wait_ge(s["tiles_summed"], layer * NS + at_ + UB // 2)
                        sc.copy(idx[:, half * UB // 2:(half + 1) * UB // 2], srcs[:, bass.ds(at_, UB // 2)])\
                            .then_inc(s["idx_ready"], 1)

            with act.Fori(0, 2) as layer:
                sage_indices(layer)
                with act.Fori(0, NCH) as it:
                    c = layer * NCH + it
                    act.wait_ge(s["products"], (c + NCH) * 4 + 1)
                    for k, wins in enumerate(QUADS):
                        act.wait_ge(s["h_transposed"], c * 2 + k + 1 + 1)
                        alone(act)
                        sc.activation(hT[:, wins[0]:wins[-1] + 1, :], ps_tr[:, wins[0]:wins[-1] + 1, :], ACT.Relu,
                                      bias=blT_sb[:, bass.ds(layer, 1)]).then_inc(s["h_copied"], 1)
                    act.wait_ge(s["y_free"], c + NCH)
                    for b in (0, 2):
                        act.wait_ge(s["products"], (c + NCH) * 4 + b + 1 + 1)
                        w, n = PAIRS[b][0], len(PAIRS[b])
                        sc.copy(y_staged(it % 2, w, n), ps_prod[:, w:w + n, 0:F])
                        sc.copy(res[:, bass.ds(it * (CW * F) + w * F, n * F)].rearrange("p (u f) -> p u f", f=F),
                                ps_prod[:, w:w + n, F:2 * F]).then_inc(s["prod_act"], 1)
            sage_indices(2)
            act.preload_act_table_set("natural_log_exp_and_others")

            with act.Fori(0, NCH) as it:
                act.wait_ge(s["z_var"], it + 1)
                sc.activation(rs[:, :], ve[:, :], ACT.Ln).then_inc(s["z_rs"], 1)
                act.wait_ge(s["z_rs"], it * 2 + 1)
                sc.activation(rs[:, :], rs[:, :], ACT.Exp, scale=-0.5).then_inc(s["z_rs"], 1)
                act.wait_ge(s["x1_prod"], it * 4 + 1)
                for k, wins in enumerate(QUADS):
                    act.wait_ge(s["x1_tr"], it * 2 + k + 1 + 1)
                    sc.copy(hT[:, wins[0]:wins[-1] + 1, :], ps_tr[:, wins[0]:wins[-1] + 1, :]).then_inc(s["x1_copied"], 1)
                act.wait_ge(s["q_free"], it + 1)
                for b, wins in enumerate(PAIRS):
                    n = len(wins)
                    act.wait_ge(s["x1_prod"], it * 4 + b + 1 + 1)
                    sc.copy(q_staged(it % 2, wins[0], n),
                            ps[:, 2 + b % 2, 0:n * 2 * F].rearrange("p (u f) -> p u f", f=2 * F)).then_inc(s["q_staged"], 1)

            def ok(g):
                return not isinstance(g, int) or 0 <= g < NG

            def indices(g, slot):
                act.wait_ge(s["added"], g + 1)
                sc.copy(idx[:, slot * G:(slot + 1) * G], srcs[:, bass.ds(g * G, G)]).then_inc(s["qi"], 1)

            def conv_step(j, slot):
                g = j - 2
                if ok(g):
                    act.wait_ge(s["added"], g + 5)
                    if not isinstance(g, int) or g >= 1:
                        act.wait_ge(s["spd"], g)
                    log_ = lg[:, slot % 2, :, :]
                    sc.activation(log_, pre[:, slot % 2, :, :], ACT.Abs).then_inc(s["absd"], 1)
                if ok(j - 3):
                    act.wait_ge(s["diffd"], j - 3 + 2)
                    sc.activation(sg, sg, ACT.Exp).then_inc(s["sigd"], 1)
                if ok(g):
                    act.wait_ge(s["absd"], g + 1)
                    sc.activation(log_, log_, ACT.Exp, scale=-1.0).then_inc(s["expd"], 1)
                    act.wait_ge(s["expd"], g + 1)
                    sc.activation(log_, log_, ACT.Ln, bias=1.0).then_inc(s["logd"], 1)
                if ok(j + 2) and ok(j):
                    indices(j + 2, (slot + 2) % GB)
                if ok(j):
                    act.wait_ge(s["oh_tr"], j + 1)
                    act.wait_ge(s["pre_ready"], j + 3)
                    sc.copy(ohT[:, slot % 2, :, :], ps_ohT[:, slot % 2, :, :]).then_inc(s["oh_copied"], 1)

            act.wait_ge(s["q_written"], NCH * 16)
            act.wait_ge(s["x_kept"], NCH + 1)
            indices(0, 0)
            indices(1, 1)
            for j in range(GB):
                conv_step(j, j)
            with act.Fori(1, NG // GB - 1) as m:
                for g in range(GB):
                    conv_step(m * GB + g, g)
            for j in range(NG - GB, NG + GB):
                conv_step(j, j % GB)
            for i, w in enumerate(range(0, NW, 4)):
                n = min(4, NW - w)
                act.wait_ge(s["cen_ready"], i + 1)
                if i >= 2:
                    act.wait_ge(s["sq_used"], i - 1)
                sc.activation(work[:, 5376 + i % 2 * 512:5376 + i % 2 * 512 + n * F], cen[:, w * F:(w + n) * F],
                              ACT.Square).then_inc(s["sq_ready"], 1)
            act.wait_ge(s["bv_var"], 1)
            sc.activation(small[:, 1, :], small[:, 0, :], ACT.Ln).then_inc(s["bv_rs"], 1)
            act.wait_ge(s["bv_rs"], 1)
            sc.activation(small[:, 1, :], small[:, 1, :], ACT.Exp, scale=-0.5).then_inc(s["bv_rs"], 1)
            with act.Fori(0, 2 * NCH) as i:
                act.wait_ge(s["t_var"], i + 1)
                sc.activation(rs[:, :], ve[:, :], ACT.Ln).then_inc(s["t_rs"], 1)
                act.wait_ge(s["t_rs"], i * 2 + 1)
                sc.activation(rs[:, :], rs[:, :], ACT.Exp, scale=-0.5).then_inc(s["t_rs"], 1)

        @block.vector
        def _(dve):
            v = nc.vector
            chain = [0]
            base_chain = [0]

            def link(ins):
                chain[0] += 1
                ins.then_inc(s["dve"], 1)
                dve.wait_ge(s["dve"], base_chain[0] + chain[0])

            def in_loop(i, per_turn, before):
                base_chain[0] = before + i * per_turn
                chain[0] = 0

            S0, S_, AF, BF, NE, NN, ONE, C50, D50, DD, IND, KR, TK, WK, W128, JK = range(16)

            def row(r, a=0, b=NB):
                return sch[:, r, a:b]

            v.memset(zero[:, :], 0.0)
            link(v.memset(sch[:, :, :], 0.0))
            dve.wait_ge(s["dnat"], 16)
            link(v.tensor_copy(d_f, d_nat))
            link(v.tensor_tensor(junk, d_f[:, 1:NT + 1], d_f[:, 0:NT], ALU.subtract))
            link(v.tensor_reduce(sch[:, TK, 0:1], junk, X, ALU.min))
            link(v.tensor_scalar(sch[:, S0, NB:NB + 1], sch[:, TK, 0:1], 0.0, None, ALU.is_lt))
            link(v.tensor_single_scalar(d_nat[:, 0:NT], d_nat[:, 0:NT], 7, ALU.arith_shift_right))
            link(v.tensor_copy(d_win, d_nat[:, 0:NT]))
            for w in range(1, NB):
                ins = v.tensor_scalar(junk.bitcast(bf16)[:, 0:NT], d_win, float(w), None, ALU.is_lt, ALU.add,
                                      accum_out=sch[:, S0, w:w + 1])
                if w < NW:
                    link(ins)
            ins.then_inc(s["cnt"], 1)
            dve.wait_ge(s["S"], 1)
            link(v.tensor_copy(row(S_, 0, NB + 1), ps[:, 6, 0:NB + 1]))
            v.tensor_copy(flag[:, :], sch[:, S_, NB:NB + 1])
            v.tensor_copy(schi[:, 0, 0:NB], row(S_))
            link(v.tensor_scalar(row(AF), row(S_), -1.0, None, ALU.add))
            v.tensor_copy(schi[:, 1, 0:NB], row(AF))
            link(v.memset(row(ONE), 1.0))
            link(v.tensor_single_scalar(schi[:, 2:4, 0:NB], schi[:, 0:2, 0:NB], 7, ALU.arith_shift_right))
            v.tensor_copy(row(AF), schi[:, 2, 0:NB])
            link(v.tensor_copy(row(BF), schi[:, 3, 0:NB]))
            link(v.tensor_tensor(row(NN, 0, NW), row(BF, 1, NB), row(AF, 0, NW), ALU.subtract))
            link(v.tensor_tensor(row(NE, 0, NW), row(S_, 1, NB), row(S_, 0, NW), ALU.is_gt))
            link(v.scalar_tensor_tensor(out=row(NN, 0, NW), in0=row(NN, 0, NW), scalar=1.0, in1=row(NE, 0, NW),
                                        op0=ALU.add, op1=ALU.mult))
            link(v.tensor_tensor_scan(row(C50, 1, NB), row(ONE, 0, NW), row(NN, 0, NW), 0.0, ALU.mult, ALU.add))
            link(v.tensor_tensor(row(D50), row(AF), row(C50), ALU.subtract))
            link(v.tensor_tensor(row(DD, 0, NW), row(D50, 1, NB), row(D50, 0, NW), ALU.subtract))
            dve.wait_ge(s["const"], 9)
            for c in range(NC):
                link(v.tensor_scalar(row(IND, 0, NW), row(C50, 1, NB), kcol[:, c:c + 1], None, ALU.is_le, ALU.add,
                                     accum_out=sch[:, WK, c:c + 1]))
                link(v.tensor_tensor_reduce(out=row(JK, 0, NW), in0=row(IND, 0, NW), in1=row(DD, 0, NW), scale=1.0,
                                            scalar=0.0, op0=ALU.mult, op1=ALU.add, accum_out=sch[:, TK, c:c + 1]))
            link(v.tensor_tensor(sch[:, TK, 0:NC], sch[:, TK, 0:NC], kcol[:, :], ALU.add))
            link(v.tensor_scalar(sch[:, TK, 0:NC], sch[:, TK, 0:NC], float(NT - 1), 0.0, ALU.min, ALU.max))
            v.tensor_copy(tki[:, :], sch[:, TK, 0:NC]).then_inc(s["tki"], 1)
            v.tensor_scalar(sch[:, W128, 0:NC], sch[:, WK, 0:NC], float(P), None, ALU.mult)
            v.tensor_scalar(tabf[:, 0, :], sch[:, WK, 0:NC], float(NW - 1), float(FA), ALU.min, ALU.mult)
            v.tensor_scalar(tabf[:, 1, :], sch[:, WK, 0:NC], float(NW - 1), float(2 * F), ALU.min, ALU.mult)
            link(v.tensor_scalar(tabf[:, 2, :], sch[:, TK, 0:NC], float(P), None, ALU.mult))
            v.tensor_copy(tabi[:, :, :], tabf[:, :, :]).then_inc(s["tab"], 1)
            dve.wait_ge(s["tki"], 1)
            unsorted = dve.value_load(flag[0:1, 0:1], min_val=0, max_val=P)
            link(v.tensor_copy(f_base[:, 0:NB], row(S_)))
            with dve.If(unsorted > 0):
                with dve.Fori(0, NT) as t:
                    dve.wait_ge(s["fl"], (t + 1) * 48)
                    f0 = s["f_done"]
                    v.tensor_single_scalar(fhi[:, :], fd[:, :], 7, ALU.arith_shift_right).then_inc(f0, 1)
                    dve.wait_ge(f0, t * 6 + 1)
                    v.tensor_copy(fcol[:, 0:1], fhi[:, :]).then_inc(f0, 1)
                    dve.wait_ge(f0, t * 6 + 2)
                    v.tensor_scalar(fcol[:, 1:2], fcol[:, 0:1], float(NW), None, ALU.min).then_inc(f0, 1)
                    dve.wait_ge(f0, t * 6 + 3)
                    v.tensor_scalar(f_oh[:, 0:NB], iota[:, 0:NB], fcol[:, 1:2], None, ALU.is_equal)\
                        .then_inc(s["f_onehot"], 1)
                    dve.wait_ge(s["f_rank"], t + 1)
                    v.tensor_tensor(f_tmp[:, 0:NB], ps[:, 6, 0:NB], f_base[:, 0:NB], ALU.add).then_inc(f0, 1)
                    dve.wait_ge(f0, t * 6 + 4)
                    v.tensor_tensor_reduce(out=row(JK), in0=f_tmp[:, 0:NB], in1=f_oh[:, 0:NB], scale=1.0, scalar=0.0,
                                           op0=ALU.mult, op1=ALU.add, accum_out=fcol[:, 2:3]).then_inc(f0, 1)
                    v.tensor_tensor(f_base[:, 0:NB], ps[:, 7, 0:NB], f_base[:, 0:NB], ALU.add).then_inc(f0, 1)
                    dve.wait_ge(f0, t * 6 + 6)
                    v.tensor_copy(fpos[:, :], fcol[:, 2:3]).then_inc(s["f_pos"], 1)
            dve.wait_ge(s["products"], NCH * 4 + 1)
            v.memset(acc[:, :], 0.0).then_inc(s["acc_clear"], 1)
            dve.wait_ge(s["rows"], 2 * NC * 16)
            for c in range(NC):
                v.tensor_scalar(d_rowsf[:, c * P:(c + 1) * P], d_rows[:, c * P:(c + 1) * P],
                                sch[:, W128, c:c + 1], None, ALU.subtract)
            v.tensor_copy(s_rowsf, s_rows).then_inc(s["rowsf"], 1)
            dve.wait_ge(s["rows_tr"], 1)
            v.tensor_copy(srcs[:, :], ps_tr[:, 8:8 + NC, :].rearrange("p c e -> p (c e)")).then_inc(s["srcs_ready"], 1)
            dve.wait_ge(s["dlo_ready"], 1)
            dve.wait_ge(s["tab_back"], 64)
            dve.wait_ge(s["acc_clear"], 1)
            dve.wait_ge(s["loads"], LOADS * 16)
            w_regs = [dve.alloc_register(f"dve_w{u}") for u in range(UB)]
            a3 = acc[:, :].rearrange("p (w f) -> p w f", f=FA)

            def load_windows(first):
                dve.reg_load(w_regs, regs[0:1, bass.ds(first, UB)])
                return [dve.snap(r, min_val=0, max_val=(NW - 1) * FA) for r in w_regs]

            def sage_adds(layer):
                with dve.Fori(0, NS // UB) as it:
                    wins = load_windows(it * UB)
                    first = layer * NS + it * UB

                    def onehot(u):
                        dve.wait_ge(s["tiles_summed"], first + u + 13)
                        v.tensor_scalar(oh4[:, u % 4, :], iota[:, :], dlo[:, bass.ds(it * UB + u, 1)], None,
                                        ALU.is_equal).then_inc(s["onehots"], 1)

                    onehot(0)
                    onehot(1)
                    for u in range(UB):
                        if u + 2 < UB:
                            onehot(u + 2)
                        dve.wait_ge(s["tiles_summed"], first + u + 17)
                        dve.wait_ge(s["tiles_added"], first + u + 4)
                        a = acc[:, bass.ds(wins[u], FA)]
                        v.tensor_tensor(a, a, ps[:, u % 4, 0:FA], ALU.add).then_inc(s["tiles_added"], 1)

            def inverse_counts(layer):
                dve.wait_ge(s["tiles_added"], (layer + 1) * NS + 4)
                link(v.tensor_scalar(cnt[:, :], a3[:, :, F], 1.0, None, ALU.max))
                link(v.reciprocal(inv[:, :], cnt[:, :]))
                alone(dve)

            n_links = chain[0]
            with dve.Fori(0, 2) as layer:
                in_loop(layer, 2, n_links)
                sage_adds(layer)
                inverse_counts(layer)
                dve.wait_ge(s["prod_act"], (layer + 1) * (NCH * 2) + 1)
                dve.wait_ge(s["prod_dve"], (layer + 1) * (NCH * 2) + 1)
                alone(dve)
                def new_h(it):
                    c = layer * NCH + it
                    dve.wait_ge(s["h_transposed"], c * 2 + 1)
                    for u in range(CW):
                        w = it * CW + u
                        v.scalar_tensor_tensor(
                            out=hr[:, u, :], in0=acc[:, bass.ds(w * FA, F)], scalar=inv[:, bass.ds(w, 1)],
                            in1=res[:, bass.ds(w * F, F)], op0=ALU.mult, op1=ALU.add).then_inc(s["h_ready"], 1)
                    dve.wait_ge(s["h_ready"], (c + 1) * CW)
                    v.tensor_copy(acc[:, bass.ds(it * (CW * FA), CW * FA)], zero[:, :].to_broadcast([P, CW * FA]))\
                        .then_inc(s["acc_clear"], 1)

                def copy_products(it):
                    c = layer * NCH + it
                    dve.wait_ge(s["y_free"], c + NCH)
                    for b in (1, 3):
                        dve.wait_ge(s["products"], (c + NCH) * 4 + b + 1 + 1)
                        w, n = PAIRS[b][0], len(PAIRS[b])
                        v.tensor_copy(y_staged(it % 2, w, n), ps_prod[:, w:w + n, 0:F])
                        v.tensor_copy(res[:, bass.ds(it * (CW * F) + w * F, n * F)].rearrange("p (u f) -> p u f", f=F),
                                      ps_prod[:, w:w + n, F:2 * F]).then_inc(s["prod_dve"], 1)

                new_h(0)
                with dve.Fori(1, NCH) as it:
                    new_h(it)
                    copy_products(it - 1)
                copy_products(NCH - 1)
                dve.wait_ge(s["acc_clear"], (layer + 1) * NCH + 1)
            n_links += 4
            in_loop(0, 0, n_links)
            link(v.tensor_tensor(x_sb[:, :].rearrange("p (u f) -> p u f", f=F),
                                 x_sb[:, :].rearrange("p (u f) -> p u f", f=F),
                                 bl2[:, :].unsqueeze(1).to_broadcast([P, NW, F]), ALU.add))
            sage_adds(2)
            inverse_counts(2)
            dve.wait_ge(s["prod_act"], 3 * NCH * 2 + 1)
            dve.wait_ge(s["prod_dve"], 3 * NCH * 2 + 1)
            n_links += 3

            def layer_norm(src_, dst_, var_sem, rs_sem, n):
                for u in range(CW):
                    last = v.bn_stats(st6[:, u, :], src_[:, u, :])
                link(last)
                alone(dve)
                for u in range(CW):
                    last = v.bn_aggr(mv[:, u, :], st6[:, u, :])
                link(last)
                v.tensor_scalar(ve[:, :], mv[:, :, 1], EPS, None, ALU.add).then_inc(s[var_sem], 1)
                dve.wait_ge(s[var_sem], n + 1)
                dve.wait_ge(s[rs_sem], (n + 1) * 2)
                newton(rs[:, :], ve[:, :], rt[:, :])
                for u in range(CW):
                    last = v.tensor_scalar(dst_[:, u, :], src_[:, u, :], mv[:, u, 0:1], rs[:, u:u + 1],
                                           ALU.subtract, ALU.mult)
                return last

            def newton(y, var_, t):
                link(v.tensor_tensor(t, y, y, ALU.mult))
                link(v.tensor_tensor(t, t, var_, ALU.mult))
                link(v.tensor_scalar(t, t, -0.5, 1.5, ALU.mult, ALU.add))
                link(v.tensor_tensor(y, y, t, ALU.mult))

            per = 8
            def new_x1(it):
                in_loop(it, per, n_links)
                dve.wait_ge(s["x1_tr"], it * 2 + 1)
                dve.wait_ge(s["x_kept"], it + 1)
                for u in range(CW):
                    w = it * CW + u
                    last = v.scalar_tensor_tensor(
                        out=hr[:, u, :], in0=acc[:, bass.ds(w * FA, F)], scalar=inv[:, bass.ds(w, 1)],
                        in1=res[:, bass.ds(w * F, F)], op0=ALU.mult, op1=ALU.add)
                link(last)
                link(v.tensor_tensor(hr, hr, chunk(x_sb, it, F), ALU.add))
                layer_norm(hr, hr, "z_var", "z_rs", it).then_inc(s["x1_ready"], 1)
                v.tensor_copy(acc[:, bass.ds(it * (CW * FA), CW * FA)], zero[:, :].to_broadcast([P, CW * FA]))\
                    .then_inc(s["acc_clear"], 1)
                assert chain[0] == per, chain[0]

            def add_b1(it):
                for b, wins in enumerate(PAIRS):
                    n = len(wins)
                    dve.wait_ge(s["x1_prod"], it * 4 + b + 1 + 1)
                    v.tensor_tensor(
                        pq[:, bass.ds(it * (CW * 2 * F) + wins[0] * 2 * F, n * 2 * F)].rearrange("p (u f) -> p u f", u=n),
                        ps[:, P_BANKS[b], 0:n * 2 * F].rearrange("p (u f) -> p u f", u=n),
                        b1_sb[:, :].unsqueeze(1).to_broadcast([P, n, 2 * F]), ALU.add).then_inc(s["p_done"], 1)

            new_x1(0)
            with dve.Fori(1, NCH) as it:
                new_x1(it)
                add_b1(it - 1)
            add_b1(NCH - 1)
            n_links += per * NCH
            dve.wait_ge(s["acc_clear"], 3 * NCH + 1)
            dve.wait_ge(s["x_kept"], NCH + 1)
            dve.wait_ge(s["q_written"], NCH * 16)

            def ok(g):
                return not isinstance(g, int) or 0 <= g < NG

            def conv_step(j, slot, m, wins):

                def add_sum(t):
                    g = j - 4
                    if ok(g):
                        if t == 0:
                            dve.wait_ge(s["agg"], g + 5)
                        dve.wait_ge(s["agg_added"], g * G + t + 8)
                        a = acc[:, bass.ds(wins[slot * G + t], F)]
                        v.tensor_tensor(a, a, ps_agg[:, slot % 2, t, :], ALU.add).then_inc(s["agg_added"], 1)

                g = j - 2
                if ok(g):
                    dve.wait_ge(s["pre_ready"], g + 5)
                    turn = g // GB if isinstance(g, int) else m - (1 if slot < 2 else 0)
                    dve.wait_ge(s_qg[(slot - 2) % GB], (turn + 1) * 64)
                    if not isinstance(g, int) or g >= 1:
                        dve.wait_ge(s["spd"], g)
                        dve.wait_ge(s["diffd"], g)
                    v.tensor_tensor(pre[:, slot % 2, :, :], ps_pre[:, slot % 2, :, :], qg[:, (slot - 2) % GB, :, :],
                                    ALU.add).then_inc(s["added"], 1)
                add_sum(0)
                g = j - 3
                pre_, log_ = pre[:, (slot - 3) % 2, :, :], lg[:, (slot - 3) % 2, :, :]
                if ok(g):
                    dve.wait_ge(s["logd"], g + 1)
                    dve.wait_ge(s["msgd"], g + 1)
                    v.scalar_tensor_tensor(out=sg, in0=pre_[:, :, 0:F], scalar=0.0, in1=log_[:, :, 0:F],
                                           op0=ALU.min, op1=ALU.subtract).then_inc(s["diffd"], 1)
                add_sum(1)
                if ok(g):
                    v.scalar_tensor_tensor(out=sp_, in0=pre_[:, :, F:2 * F], scalar=0.0, in1=log_[:, :, F:2 * F],
                                           op0=ALU.max, op1=ALU.add).then_inc(s["spd"], 1)
                add_sum(2)
                if ok(j):
                    dve.wait_ge(s["agg"], j + 1)
                    v.tensor_tensor(oh[:, slot, :, :], iota[:, :].unsqueeze(1).to_broadcast([P, G, P]),
                                    dlo[:, bass.ds(j * G, G)].unsqueeze(2).to_broadcast([P, G, P]), ALU.is_equal)\
                        .then_inc(s["oh1"], 1)
                add_sum(3)
                if ok(g):
                    dve.wait_ge(s["sigd"], g + 1)
                    dve.wait_ge(s["spd"], g + 2)
                    dve.wait_ge(s["agg"], g + 3)
                    v.tensor_tensor(mm[:, (slot - 3) % 2, :, :], sg, sp_, ALU.mult).then_inc(s["msgd"], 1)

            for j in range(GB):
                conv_step(j, j, 0, None)
            with dve.Fori(1, NG // GB) as m:
                wins = load_windows(m * UB - UB)
                for g in range(GB):
                    conv_step(m * GB + g, g, m, wins)
            wins = load_windows(NS - UB)
            for j in range(NG, NG + GB):
                conv_step(j, j % GB, NG // GB, wins)
            in_loop(0, 0, n_links)
            dve.wait_ge(s["bn_sum"], 1)
            link(v.tensor_reduce(small[:, 2, :], ps[:, 0, :].rearrange("p (a f) -> p f a", f=F), X, ALU.add))
            link(v.tensor_scalar(mean[:, :], small[:, 2, :], 1.0 / N, None, ALU.mult))
            for w in range(0, NW, 4):
                n = min(4, NW - w)
                v.tensor_tensor(cen[:, w * F:(w + n) * F].rearrange("p (u f) -> p u f", f=F), a3[:, w:w + n, 0:F],
                                mean[:, :].unsqueeze(1).to_broadcast([P, n, F]), ALU.subtract).then_inc(s["cen_ready"], 1)
            NQ = -(-NW // 4)
            dve.wait_ge(s["sq_used"], NQ)
            link(v.tensor_reduce(small[:, 3, :], ps[:, 1, :].rearrange("p (a f) -> p f a", f=F), X, ALU.add))
            v.tensor_scalar(small[:, 0, :], small[:, 3, :], 1.0 / N, EPS, ALU.mult, ALU.add).then_inc(s["bv_var"], 1)
            dve.wait_ge(s["bv_var"], 1)
            dve.wait_ge(s["bv_rs"], 2)
            newton(small[:, 1, :], small[:, 0, :], small[:, 2, :])
            v.tensor_tensor(bscale[:, :], small[:, 1, :], bn_sb[:, 0, :], ALU.mult).then_inc(s["bv_rs"], 1)
            n_links += chain[0]
            per = 17
            with dve.Fori(0, NCH) as it:
                in_loop(it, per, n_links)
                xc = chunk(x_sb, it, F)
                dve.wait_ge(s["t_scaled"], (it + 1) * 2)
                dve.wait_ge(s["o_ready"], it + 1)
                v.tensor_tensor(tmp2, tmp, xc, ALU.add).then_inc(s["t_used"], 1)
                dve.wait_ge(s["t_used"], it + 1 + 1)
                link(layer_norm(tmp2, tmp2, "t_var", "t_rs", it * 2))
                link(v.tensor_tensor(tmp2, tmp2, bn_sb[:, 2, :].unsqueeze(1).to_broadcast([P, CW, F]), ALU.mult))
                link(v.tensor_tensor(tmp2, tmp2, bn_sb[:, 3, :].unsqueeze(1).to_broadcast([P, CW, F]), ALU.add))
                link(v.scalar_tensor_tensor(out=tmp2, in0=tmp2, scalar=0.0, in1=xc, op0=ALU.max, op1=ALU.add))
                link(v.tensor_tensor(tmp2, tmp2, xc, ALU.add))
                dve.wait_ge(s["o_free"], it + 1)
                layer_norm(tmp2, hr, "t_var", "t_rs", it * 2 + 1).then_inc(s["o_ready"], 1)
                per_now = chain[0]
            assert per_now == per, per_now


_INS = ["x", "xT", "src", "dst", "ea", "eaT", "w0", "bl", "blT", "w1", "we", "b1", "bn"]


def kernel(**inputs):
    import numpy as np
    import concourse.bacc as bacc
    from concourse.bass_utils import run_bass_kernel_spmd

    a = {k: np.asarray(v) for k, v in inputs.items()}
    f = np.float32

    def padded(v, n, fill=0):
        return np.concatenate([v, np.full((n - v.shape[0],) + v.shape[1:], fill, v.dtype)])

    x = padded(a["x"], NP)
    ea = padded(a["edge_attr_16"], EP)
    wf, ws = a["L1_gnn_Wf"].T, a["L1_gnn_Ws"].T
    arrays = {
        "x": x, "xT": x.T,
        "src": padded(a["src"], EP), "dst": padded(a["dst"], EP + P, PAD),
        "ea": ea, "eaT": ea.T,
        "w0": np.concatenate([a["L0_gnn_Wl"], a["L0_gnn_Wr"]], axis=2),
        "bl": a["L0_gnn_bl"], "blT": a["L0_gnn_bl"].T,
        "w1": np.concatenate([wf[0:F], ws[0:F], wf[F:2 * F], ws[F:2 * F]], axis=1),
        "we": np.concatenate([wf[2 * F:], ws[2 * F:]], axis=1),
        "b1": np.concatenate([a["L1_gnn_bf"], a["L1_gnn_bs"]]),
        "bn": np.concatenate([a["L1_gnn_bn_gamma"], a["L1_gnn_bn_beta"], a["L1_gnn_ln_gamma"], a["L1_gnn_ln_beta"]]),
    }
    nc = bacc.Bacc("TRN2", target_bir_lowering=False, num_devices=1)
    ins, args = {}, []
    for name in _INS:
        v = np.ascontiguousarray(arrays[name])
        ins[f"in_{name}"] = v
        args.append(nc.dram_tensor(f"in_{name}", v.shape, mybir.dt.from_np(v.dtype), kind="ExternalInput").ap())
    out = nc.dram_tensor("out", (N, F), mybir.dt.from_np(np.dtype(f)), kind="ExternalOutput").ap()
    build_gnn(nc, *args, out)
    r = run_bass_kernel_spmd(nc, [ins], core_ids=[0])
    return r.results[0]["out"]
```

```python
import concourse.bass as bass
from concourse import mybir
from concourse.alu_op_type import AluOpType as ALU
from contextlib import ExitStack

P = 128
N = 6250
E = 100000
F = 128
ED = 16
NW = -(-N // P)
NP = NW * P
NT = -(-E // P)
EP = NT * P
G = 4
UB = 16
GB = UB // G
NS = -(-(NT + NW - 1) // UB) * UB
NG = NS // G
NC = -(-NS // P)
CW = 7
NCH = NW // CW
FA = F + 1
EA_TURNS = 46
EA_C = EP * ED // P // EA_TURNS
EA_GROUPS = [(0, 0), (0, 1), (0, 2), (1, 0), (1, 1), (1, 2), (2, 0), (2, 1)]
PAD = 1 << 20
EPS = 1e-5
assert EP * ED == P * EA_TURNS * EA_C and EA_TURNS < NS // UB
assert NW == CW * NCH and EP == P * NT


def build_gnn(nc, x, xT, src, dst, ea, eaT, w0, bl, blT, w1, we, b1, bn, out):
    f32, i32, bf16 = mybir.dt.float32, mybir.dt.int32, mybir.dt.bfloat16
    ACT = mybir.ActivationFunctionType
    X = mybir.AxisListType.X
    ctx = ExitStack()
    with ctx:
        def sb(name, shape, dt=f32):
            return ctx.enter_context(nc.sbuf_tensor(name, shape, dt))

        def sem(name):
            return ctx.enter_context(nc.semaphore(name))

        def dram(name, shape, dt=f32):
            return nc.dram_tensor(name, shape, dt).ap()

        def every_partition(row, n):
            return bass.AP(row.tensor, row.offset, [[0, P], [1, n]])

        y_dram = dram("y_dram", (NP, F))
        q_dram = dram("q_dram", (NP, 2 * F))
        dst_sorted = dram("dst_sorted", (NT, P), i32)
        src_sorted = dram("src_sorted", (NT, P), i32)
        eaT_sorted = dram("eaT_sorted", (ED, EP))
        ea_parts = dram("ea_parts", (len(EA_GROUPS) * ED, EP), bf16)
        regs_dram = dram("regs_dram", (3, NC * P), i32)
        fb_dst = dram("fb_dst", (EP, 1), i32)
        fb_src = dram("fb_src", (EP, 1), i32)
        fb_ea = dram("fb_ea", (EP, ED))

        x_sb = sb("x_sb", [P, NW * F])
        acc = sb("acc", [P, NW * FA])
        pq = sb("pq", [P, NW * 2 * F])
        r_off = NW * F
        res = pq[:, r_off:2 * r_off]
        dlo = sb("dlo", [P, NC * P])
        srcs = sb("srcs", [P, NC * P], i32)
        regs = sb("regs", [1, 3 * NC * P], i32)
        xT_sb = acc[:, 0:NW * F]
        zero = sb("zero", [P, 1])
        iota = sb("iota", [P, P])
        ident = sb("ident", [P, P])
        ones = sb("ones", [P, P])
        mask = sb("mask", [P, P])
        w0_sb = sb("w0_sb", [P, 3, 2 * F])
        w1_sb = sb("w1_sb", [P, 4 * F])
        we_sb = sb("we_sb", [ED, 2 * F])
        we_part = sb("we_part", [ED, 3, 2 * F], bf16)
        we_rows = sb("we_rows", [P, 2 * F], bf16)
        blT_sb = sb("blT_sb", [P, 3])
        bl2 = sb("bl2", [P, F])
        b1_sb = sb("b1_sb", [P, 2 * F])
        bn_sb = sb("bn_sb", [P, 4, F])
        inv = sb("inv", [P, NW])
        cnt = sb("cnt", [P, NW])

        gath = sb("gath", [P, UB, 2 * F])
        msg = gath[:, :, 0:FA]
        qg = gath[:, :, :].rearrange("p (g t) f -> p g t f", t=G)
        idx = sb("idx", [P, UB], i32)

        work = sb("work", [P, 9728])
        hr = work[:, 0:896].rearrange("p (u f) -> p u f", f=F)
        hT = work[:, 896:1792].rearrange("p (u f) -> p u f", f=F)
        Y_STAGE = Q_STAGE = 2 * CW * F
        oh4 = work[:, 3584:4096].rearrange("p (u f) -> p u f", f=P)
        tmp = work[:, 3584:4480].rearrange("p (u f) -> p u f", f=F)
        tmp2 = work[:, 4480:5376].rearrange("p (u f) -> p u f", f=F)
        x1c = work[:, 5376:6272].rearrange("p (u f) -> p u f", f=F)
        oh = work[:, 0:2048].rearrange("p (g t f) -> p g t f", g=GB, t=G)
        ohT = work[:, 2048:3072].rearrange("p (g t f) -> p g t f", g=2, t=G)
        pre = work[:, 3072:5120].rearrange("p (g t f) -> p g t f", g=2, t=G)
        lg = work[:, 5120:7168].rearrange("p (g t f) -> p g t f", g=2, t=G)
        sg = work[:, 7168:7680].rearrange("p (t f) -> p t f", t=G)
        sp_ = work[:, 7680:8192].rearrange("p (t f) -> p t f", t=G)
        mm = work[:, 8192:9216].rearrange("p (g t f) -> p g t f", g=2, t=G)
        ea_sb = sb("ea_sb", [P, UB, P], bf16)
        mean = sb("mean", [P, F])
        bscale = sb("bscale", [P, F])
        small = sb("small", [P, 4, F])
        st6 = sb("st6", [P, CW, 6])
        mv = sb("mv", [P, CW, 2])
        ve = sb("ve", [P, CW])
        rs = sb("rs", [P, CW])
        rt = sb("rt", [P, CW])
        nm = sb("nm", [P, CW])
        st_a, st_b = sb("st_a", [P, CW, 6]), sb("st_b", [P, CW, 6])
        mv_a, mv_b = sb("mv_a", [P, CW, 2]), sb("mv_b", [P, CW, 2])
        ve_a, ve_b = sb("ve_a", [P, CW]), sb("ve_b", [P, CW])
        rs_a, rs_b = sb("rs_a", [P, CW]), sb("rs_b", [P, CW])
        nm_a, nm_b = sb("nm_a", [P, CW]), sb("nm_b", [P, CW])
        cen = pq[:, 0:NW * F]

        at = [0]

        def part(n, dt=f32):
            v = pq[:, at[0]:at[0] + n]
            at[0] += n
            return v if dt == f32 else v.bitcast(dt)

        d_nat = part(NT + 1, i32)
        d_f = part(NT + 1)
        junk = part(NT)
        d_win = work[:, 5376:5376 + NT // 2].bitcast(bf16)
        d_rows = part(NC * P, i32)
        s_rows = part(NC * P, i32)
        d_rowsf = part(NC * P)
        s_rowsf = part(NC * P)
        assert at[0] <= r_off
        ea_part = [pq[:, 1024 + k * EA_C // 2:1024 + (k + 1) * EA_C // 2].bitcast(bf16) for k in range(3)]

        def ea_chunk(n):
            return pq[:, bass.ds(n % 2 * EA_C, EA_C)]

        NB = NW + 1
        sch = sb("sch", [P, 20, 52])
        schi = sb("schi", [P, 4, 52], i32)
        kcol = sb("kcol", [P, NC])
        tki = sb("tki", [P, NC], i32)
        tabf = sb("tabf", [P, 3, NC])
        tabi = sb("tabi", [P, 3, NC], i32)
        flag = sb("flag", [P, 1], i32)
        tri = sb("tri", [P, P])
        fd = sb("fd", [P, 1], i32)
        fs = sb("fs", [P, 1], i32)
        fe = sb("fe", [P, ED])
        fhi = sb("fhi", [P, 1], i32)
        fpos = sb("fpos", [P, 1], i32)
        fcol = sb("fcol", [P, 4])
        f_oh = sb("f_oh", [P, 52])
        f_tmp = sb("f_tmp", [P, 52])
        f_base = sb("f_base", [P, 52])

        ps = ctx.enter_context(nc.psum_tensor("ps", [P, 8, 512], f32))
        ps_prod = ps[:, 0:4, :].rearrange("p b (h f) -> p (b h) f", h=2)
        ps_tr = ps[:, 4:8, :].rearrange("p b (h f) -> p (b h) f", h=4)
        ps_pre = ps[:, 0:4, :].rearrange("p (g b) (h f) -> p g (b h) f", g=2, h=2)
        ps_ohT = ps[:, 4:6, :].rearrange("p g (t f) -> p g t f", t=G)
        ps_agg = ps[:, 6:8, :].rearrange("p g (t f) -> p g t f", t=G)

        names = """const loads dnat w0_in xT_first xT_rest y_written products dve cnt S
            tki tab tab_back idx_given idx_sorted ea_sorted rows rowsf rows_tr dlo_ready srcs_ready
            fl f_onehot f_rank f_pos f_scattered f_done
            idx_ready onehots tiles_added tiles_summed h_ready h_transposed h_copied
            prod_act prod_dve var_z rs_z coef_z x1_ready x1_tr x1_copied x1_prod p_done q_staged
            q_written x_kept acc_clear
            ea_in ea_1 ea_r1 ea_2 ea_r2 ea_3 ea_written ea_free we_split we_in
            qi oh1 oh_tr oh_copied pre_ready added absd expd logd diffd sigd spd msgd agg
            agg_added bn_sum bn_sq sq_ready sq_used cen_ready bv_var bv_rs
            passed y_free q_free o_free f_free ones_col
            h_scaled var_a rs_a coef_a normed_a a_used var_b rs_b coef_b o_ready o_written"""
        s = {n: sem("s_" + n) for n in names.split()}
        s_msg = [sem(f"s_msg{u}") for u in range(UB)]
        s_qg = [sem(f"s_qg{g}") for g in range(GB)]
        s_ea = [sem(f"s_ea{g}") for g in range(GB)]
        LOADS = 8
        FROM_ONE = ("products", "prod_act", "prod_dve", "h_copied", "x1_copied", "x1_prod", "h_transposed",
                    "x1_tr", "x_kept", "o_ready", "ea_free", "spd", "msgd", "diffd", "y_free", "o_free", "f_free")

        block = ctx.enter_context(nc.Block())

        def alone(engine):
            engine.sem_inc(s["passed"], 1)

        PAIRS = [(0, 1), (2, 3), (4, 5), (6,)]
        QUADS = [(0, 1, 2, 3), (4, 5, 6)]
        XT_PARTS = [(0, 2), (2, NCH)]
        P_BANKS = (0, 1, 6, 7)

        def y_staged(slot, w=0, n=CW):
            return work[:, bass.ds(slot * (CW * F) + (Y_STAGE + w * F), n * F)].rearrange("p (u f) -> p u f", f=F)

        def q_staged(slot, w=0, n=CW):
            return work[:, bass.ds(slot * (CW * 2 * F) + (Q_STAGE + w * 2 * F), n * 2 * F)]\
                .rearrange("p (u f) -> p u f", f=2 * F)

        def chunk(t, it, n):
            return t[:, bass.ds(it * (CW * n), CW * n)].rearrange("p (u f) -> p u f", f=n)

        @block.sync
        def _(sp):
            for name, slots in (("tiles_summed", UB), ("tiles_added", 4), ("p_done", 4), ("q_free", 2),
                                ("q_staged", 2), ("pre_ready", GB),
                                ("added", GB), ("oh_copied", 2), ("agg", GB), ("agg_added", 2 * G)):
                sp.sem_inc(s[name], slots)
            for name in FROM_ONE:
                sp.sem_inc(s[name], 1)
            d_flat = bass.AP(dst.tensor, dst.offset, [[NT, P], [1, NT + 1]])
            sp.dma_start(d_nat, d_flat).then_inc(s["dnat"], 16)
            sp.dma_start(w0_sb[:, :, :], w0.rearrange("l k n -> k l n")).then_inc(s["w0_in"], 16)
            for loaded, (c0, c1) in zip(("xT_first", "xT_rest"), XT_PARTS):
                sp.dma_start(xT_sb[:, c0 * CW * P:c1 * CW * P], xT[:, c0 * CW * P:c1 * CW * P]).then_inc(s[loaded], 16)
            d2 = dst[0:EP].rearrange("(t e) -> t e", e=P)
            s2 = src[0:EP].rearrange("(t e) -> t e", e=P)
            sp.dma_start(dst_sorted, d2).then_inc(s["idx_given"], 16)
            sp.dma_start(src_sorted, s2).then_inc(s["idx_given"], 16)
            with sp.Fori(0, NCH) as it:
                sp.wait_ge(s["prod_act"], (it + 1) * 2 + 1)
                sp.dma_start(y_dram[bass.ds(it * (CW * P), CW * P), :].rearrange("(u p) f -> p u f", p=P),
                             y_staged(it % 2)).then_inc(s["y_written"], 16)
                sp.wait_ge(s["y_written"], (it + 1) * 16)
                sp.sem_inc(s["y_free"], 1)
            sp.wait_ge(s["tki"], 1)
            unsorted = sp.value_load(flag[0:1, 0:1], min_val=0, max_val=P)
            with sp.If(unsorted > 0):
                with sp.Fori(0, NT) as t:
                    sp.wait_ge(s["f_free"], t + 1)
                    with nc.allow_non_contiguous_dma(reason="a column of indices"):
                        sp.dma_start(fd[:, :], dst[bass.ds(t * P, P)].rearrange("(e o) -> e o", o=1)).then_inc(s["fl"], 16)
                        sp.dma_start(fs[:, :], src[bass.ds(t * P, P)].rearrange("(e o) -> e o", o=1)).then_inc(s["fl"], 16)
                    sp.dma_start(fe[:, :], ea[bass.ds(t * P, P), :]).then_inc(s["fl"], 16)
                sp.wait_ge(s["f_scattered"], NT * 48)
                sp.wait_ge(s["idx_given"], 32)
                sp.dma_start(dst_sorted, fb_dst.rearrange("(t e) o -> t (e o)", e=P)).then_inc(s["idx_sorted"], 16)
                sp.dma_start(src_sorted, fb_src.rearrange("(t e) o -> t (e o)", e=P)).then_inc(s["idx_sorted"], 16)
                with nc.allow_non_contiguous_dma(reason="edge attributes transposed"):
                    for h in range(2):
                        sp.dma_start(eaT_sorted[:, h * EP // 2:(h + 1) * EP // 2],
                                     fb_ea[h * EP // 2:(h + 1) * EP // 2, :].rearrange("e k -> k e"))\
                            .then_inc(s["ea_sorted"], 16)
            sp.wait_ge(s["tab"], 1)
            with nc.allow_non_contiguous_dma(reason="the schedule, transposed"):
                for r in range(3):
                    sp.dma_start(regs_dram[r, :].rearrange("(c p) -> p c", p=P), tabi[:, r, :]).then_inc(s["tab_back"], 16)
            sp.wait_ge(s["tab_back"], 48)
            sp.dma_start(regs[:, :], regs_dram.rearrange("(o r) k -> o (r k)", o=1)).then_inc(s["tab_back"], 16)
            with sp.If(unsorted < 1):
                sp.wait_ge(s["rows"], 2 * NC * 16)
                for h in range(2):
                    sp.dma_start(eaT_sorted[:, h * EP // 2:(h + 1) * EP // 2],
                                 eaT[:, h * EP // 2:(h + 1) * EP // 2]).then_inc(s["ea_sorted"], 16)
            with sp.Fori(0, 2) as layer:
                with sp.Fori(0, NCH) as it:
                    sp.wait_ge(s["prod_act"], ((layer + 1) * NCH + it + 1) * 2 + 1)
                    sp.wait_ge(s["prod_dve"], ((layer + 1) * NCH + it + 1) * 2 + 1)
                    sp.dma_start(y_dram[bass.ds(it * (CW * P), CW * P), :].rearrange("(u p) f -> p u f", p=P),
                                 y_staged(it % 2)).then_inc(s["y_written"], 16)
                    sp.wait_ge(s["y_written"], ((layer + 1) * NCH + it + 1) * 16)
                    sp.sem_inc(s["y_free"], 1)
            sp.wait_ge(s["we_split"], 1)
            for k, (_, part_) in enumerate(EA_GROUPS):
                sp.dma_start(we_rows[k * ED:(k + 1) * ED, :], we_part[:, part_, :]).then_inc(s["we_in"], 16)
            sp.wait_ge(s["ea_sorted"], 32)
            ea_flat = eaT_sorted.rearrange("k e -> (k e)").rearrange("(p c) -> p c", p=P)
            parts_flat = ea_parts.rearrange("(g k) e -> g (k e)", k=ED).rearrange("g (p c) -> g p c", p=P)
            for n in range(2):
                sp.dma_start(ea_chunk(n), ea_flat[:, n * EA_C:(n + 1) * EA_C]).then_inc(s["ea_in"], 16)
                sp.wait_ge(s["ea_in"], (n + 1) * 16)

            def store_parts(n):
                for part_, ready in enumerate(("ea_1", "ea_2", "ea_3")):
                    sp.wait_ge(s[ready], n + 1)
                    for k, (mine, _) in enumerate(EA_GROUPS):
                        if mine == part_:
                            sp.dma_start(parts_flat[k, :, bass.ds(n * EA_C, EA_C)], ea_part[part_])\
                                .then_inc(s["ea_written"], 16)
                sp.wait_ge(s["ea_written"], (n + 1) * (16 * len(EA_GROUPS)))
                sp.sem_inc(s["ea_free"], 1)

            with sp.Fori(0, EA_TURNS - 2) as n:
                store_parts(n)
                sp.dma_start(ea_chunk(n), ea_flat[:, bass.ds((n + 2) * EA_C, EA_C)]).then_inc(s["ea_in"], 16)
                sp.wait_ge(s["ea_in"], (n + 3) * 16)
                alone(sp)
            store_parts(EA_TURNS - 2)
            store_parts(EA_TURNS - 1)
            with sp.Fori(0, NCH) as it:
                sp.wait_ge(s["q_staged"], (it + 1) * 4 + 2)
                sp.dma_start(q_dram[bass.ds(it * (CW * P), CW * P), :].rearrange("(u p) f -> p u f", p=P),
                             q_staged(it % 2)).then_inc(s["q_written"], 16)
                sp.wait_ge(s["q_written"], (it + 1) * 16)
                sp.sem_inc(s["q_free"], 1)
            tile_regs = [sp.alloc_register(f"sp_tile{u}") for u in range(UB)]
            with sp.Fori(0, NG // GB) as m:
                sp.reg_load(tile_regs, regs[0:1, bass.ds(m * UB + 2 * NC * P, UB)])
                cols = [sp.snap(r, min_val=0, max_val=EP - P) for r in tile_regs]
                for g in range(GB):
                    sp.wait_ge(s["pre_ready"], m * GB + g + 1)
                    alone(sp)
                    for t in range(G):
                        sp.dma_start(ea_sb[:, g * G + t, :], ea_parts[:, bass.ds(cols[g * G + t], P)])\
                            .then_inc(s_ea[g], 16)
            full = N // P // CW * CW
            with sp.Fori(0, NCH - 1) as it:
                sp.wait_ge(s["o_ready"], it + 1 + 1)
                sp.dma_start(out[bass.ds(it * (CW * P), CW * P), :].rearrange("(u p) f -> p u f", p=P), hr)\
                    .then_inc(s["o_written"], 16)
                sp.wait_ge(s["o_written"], (it + 1) * 16)
                sp.sem_inc(s["o_free"], 1)
            sp.wait_ge(s["o_ready"], NCH + 1)
            last = (NCH - 1) * CW * P
            nfull = (N - last) // P
            sp.dma_start(out[last:last + nfull * P, :].rearrange("(u p) f -> p u f", p=P), hr[:, 0:nfull, :])\
                .then_inc(s["o_written"], 16)
            rest = N - last - nfull * P
            sp.dma_start(out[last + nfull * P:N, :], hr[0:rest, nfull, :]).then_inc(s["o_written"], 16)
            sp.wait_ge(s["o_written"], 16 * (NCH + 1))

        @block.gpsimd
        def _(pool):
            gp = nc.gpsimd
            gp.memset(ones[:, :], 1.0).then_inc(s["const"], 1)
            gp.memset(ident[:, :], 0.0).then_inc(s["const"], 1)
            gp.memset(tri[:, :], 1.0).then_inc(s["const"], 1)
            gp.memset(mask[:, :], 1.0).then_inc(s["const"], 1)
            gp.memset(gath[:, :, F:FA], 1.0).then_inc(s["ones_col"], 1)
            gp.iota(iota[:, :], pattern=[[1, P]], base=0, channel_multiplier=0,
                    allow_small_or_imprecise_dtypes=True).then_inc(s["const"], 1)
            gp.iota(kcol[:, :], pattern=[[P, NC]], base=0, channel_multiplier=1,
                    allow_small_or_imprecise_dtypes=True).then_inc(s["const"], 1)
            pool.wait_ge(s["const"], 6)
            gp.affine_select(out=ident[:, :], in_=ident[:, :], compare_op=ALU.not_equal, fill=1.0, base=0,
                             pattern=[[-1, P]], channel_multiplier=1).then_inc(s["const"], 1)
            gp.affine_select(out=tri[:, :], in_=tri[:, :], compare_op=ALU.is_gt, fill=0.0, base=0,
                             pattern=[[1, P]], channel_multiplier=-1).then_inc(s["const"], 1)
            gp.affine_select(out=mask[:, :], in_=mask[:, :], compare_op=ALU.is_gt, fill=0.0,
                             base=N - (NW - 1) * P, pattern=[[0, P]], channel_multiplier=-1).then_inc(s["const"], 1)
            pool.wait_ge(s["tki"], 1)
            unsorted = pool.value_load(flag[0:1, 0:1], min_val=0, max_val=P)
            with pool.If(unsorted > 0):
                with pool.Fori(0, NT) as t:
                    pool.wait_ge(s["f_pos"], t + 1)
                    alone(pool)
                    off = bass.IndirectOffsetOnAxis(ap=fpos[:, 0:1], axis=0)
                    pool.indirect_dma_start(fb_dst, off, fd[:, :], None).then_inc(s["f_scattered"], 16)
                    pool.indirect_dma_start(fb_src, off, fs[:, :], None).then_inc(s["f_scattered"], 16)
                    pool.indirect_dma_start(fb_ea, off, fe[:, :], None).then_inc(s["f_scattered"], 16)
                    pool.wait_ge(s["f_scattered"], (t + 1) * 48)
                    pool.sem_inc(s["f_free"], 1)
                pool.wait_ge(s["idx_sorted"], 32)
            pool.wait_ge(s["idx_given"], 32)
            for c in range(NC):
                off = bass.IndirectOffsetOnAxis(ap=tki[:, c:c + 1], axis=0)
                pool.indirect_dma_start(d_rows[:, c * P:(c + 1) * P], None, dst_sorted, off).then_inc(s["rows"], 16)
                pool.indirect_dma_start(s_rows[:, c * P:(c + 1) * P], None, src_sorted, off).then_inc(s["rows"], 16)

            def sage_gathers(layer):
                pool.wait_ge(s["y_written"], (layer + 1) * (NCH * 16))
                alone(pool)
                with pool.Fori(0, NS // UB) as it:
                    for half in range(2):
                        pool.wait_ge(s["idx_ready"], layer * (2 * NS // UB) + it * 2 + half + 1)
                        alone(pool)
                        for u in range(half * UB // 2, (half + 1) * UB // 2):
                            pool.indirect_dma_start(
                                msg[:, u, 0:F], None, y_dram,
                                bass.IndirectOffsetOnAxis(ap=idx[:, u:u + 1], axis=0)).then_inc(s_msg[u], 16)

            with pool.Fori(0, 2) as layer:
                sage_gathers(layer)
            sage_gathers(2)
            with pool.Fori(0, NCH) as it:
                pool.wait_ge(s["x1_ready"], it + 1)
                gp.tensor_copy(chunk(x_sb, it, F), x1c).then_inc(s["x_kept"], 1)
            pool.wait_ge(s["q_written"], NCH * 16)
            with pool.Fori(0, NG // GB) as m:
                for g in range(GB):
                    pool.wait_ge(s["qi"], m * GB + g + 1)
                    alone(pool)
                    for t in range(G):
                        pool.indirect_dma_start(
                            qg[:, g, t, :], None, q_dram,
                            bass.IndirectOffsetOnAxis(ap=idx[:, g * G + t:g * G + t + 1], axis=0))\
                            .then_inc(s_qg[g], 16)
            pool.wait_ge(s["loads"], LOADS * 16)
            pool.wait_ge(s["bv_rs"], 3)
            with pool.Fori(0, NCH) as it:
                hc, xc = chunk(cen, it, F), chunk(x_sb, it, F)
                gp.tensor_tensor(hc, hc, bscale[:, :].unsqueeze(1).to_broadcast([P, CW, F]), ALU.mult)\
                    .then_inc(s["h_scaled"], 1)
                pool.wait_ge(s["h_scaled"], it * 4 + 1)
                alone(pool)
                gp.tensor_tensor(hc, hc, bn_sb[:, 1, :].unsqueeze(1).to_broadcast([P, CW, F]), ALU.add)\
                    .then_inc(s["h_scaled"], 1)
                pool.wait_ge(s["h_scaled"], it * 4 + 2)
                alone(pool)
                gp.tensor_tensor(hc, hc, xc, ALU.add).then_inc(s["h_scaled"], 1)
                pool.wait_ge(s["h_scaled"], it * 4 + 3)
                alone(pool)
                gp.tensor_tensor(xc, xc, xc, ALU.add).then_inc(s["h_scaled"], 1)

        @block.tensor
        def _(pe):
            te = nc.tensor
            pe.wait_ge(s["w0_in"], 16)

            for it in range(NCH):
                pe.wait_ge(s["xT_first" if it < XT_PARTS[0][1] else "xT_rest"], 16)
                pe.wait_ge(s["prod_act"], it * 2 + 1)
                pe.wait_ge(s["prod_dve"], it * 2 + 1)
                for b, wins in enumerate(PAIRS):
                    for u in wins:
                        w = it * CW + u
                        last = te.matmul(ps_prod[:, u, :], lhsT=xT_sb[:, w * P:(w + 1) * P], rhs=w0_sb[:, 0, :],
                                         start=True, stop=True)
                    last.then_inc(s["products"], 1)
                if it == NCH // 2:
                    pe.wait_ge(s["const"], 9)
                    pe.wait_ge(s["cnt"], 1)
                    te.matmul(ps[:, 6, 0:NB + 1], lhsT=ones[:, :], rhs=sch[:, 0, 0:NB + 1], start=True, stop=True)\
                        .then_inc(s["S"], 1)
            pe.wait_ge(s["loads"], LOADS * 16)
            pe.wait_ge(s["tki"], 1)
            unsorted = pe.value_load(flag[0:1, 0:1], min_val=0, max_val=P)
            with pe.If(unsorted > 0):
                with pe.Fori(0, NT) as t:
                    pe.wait_ge(s["f_onehot"], t + 1)
                    te.matmul(ps[:, 6, 0:NB], lhsT=tri[:, :], rhs=f_oh[:, 0:NB], start=True, stop=True)
                    te.matmul(ps[:, 7, 0:NB], lhsT=ones[:, :], rhs=f_oh[:, 0:NB], start=True, stop=True)\
                        .then_inc(s["f_rank"], 1)
            pe.wait_ge(s["rowsf"], 1)
            for c in range(2 * NC):
                rows, slot = (d_rowsf, c) if c < NC else (s_rowsf, c - NC + 8)
                last = te.transpose(ps_tr[:, slot, :], rows[:, c % NC * P:(c % NC + 1) * P], ident[:, :])
            last.then_inc(s["rows_tr"], 1)
            pe.wait_ge(s["ones_col"], 1)

            def sage_sums(layer):
                with pe.Fori(0, NS // UB) as it:
                    for u in range(UB):
                        step = layer * NS + it * UB + u
                        pe.wait_ge(s_msg[u], layer * (NS // UB * 16) + (it + 1) * 16)
                        pe.wait_ge(s["onehots"], step + 1)
                        pe.wait_ge(s["tiles_added"], step + 1)
                        te.matmul(ps[:, u % 4, 0:FA], lhsT=oh4[:, u % 4, :], rhs=msg[:, u, :],
                                  start=True, stop=True).then_inc(s["tiles_summed"], 1)

            def sage_layer(layer):
                sage_sums(layer)
                pe.wait_ge(s["tiles_added"], (layer + 1) * NS + 4)
                alone(pe)
                with pe.Fori(0, NCH) as it:
                    c = layer * NCH + it
                    for k, wins in enumerate(QUADS):
                        pe.wait_ge(s["h_ready"], c * CW + wins[-1] + 1)
                        pe.wait_ge(s["h_copied"], c * 2 + 1)
                        for u in wins:
                            last = te.transpose(ps_tr[:, u, :], hr[:, u, :], ident[:, :])
                        last.then_inc(s["h_transposed"], 1)
                    for b, wins in enumerate(PAIRS):
                        pe.wait_ge(s["h_copied"], c * 2 + b // 2 + 1 + 1)
                        pe.wait_ge(s["prod_dve"] if b % 2 else s["prod_act"], (c + NCH) * 2 + 1)
                        for u in wins:
                            last = te.matmul(ps_prod[:, u, :], lhsT=hT[:, u, :],
                                             rhs=w0_sb[:, bass.ds(layer + 1, 1), :].rearrange("p a n -> p (a n)"),
                                             start=True, stop=True)
                        last.then_inc(s["products"], 1)

            with pe.Fori(0, 2) as layer:
                sage_layer(layer)
            sage_sums(2)
            pe.wait_ge(s["tiles_added"], 3 * NS + 4)
            with pe.Fori(0, NCH) as it:
                pe.wait_ge(s["x1_ready"], it + 1)
                pe.wait_ge(s["x1_copied"], it * 2 + 1)
                for wins in QUADS:
                    for u in wins:
                        last = te.transpose(ps_tr[:, u, :], x1c[:, u, :], ident[:, :])
                    last.then_inc(s["x1_tr"], 1)
                for b, wins in enumerate(PAIRS):
                    pe.wait_ge(s["x1_copied"], it * 2 + b // 2 + 1 + 1)
                    pe.wait_ge(s["p_done"], it * 4 + b + 1)
                    pe.wait_ge(s["q_staged"], it * 4 + b + 1)
                    for h in range(2):
                        for u in wins:
                            last = te.matmul(ps[:, 2 + b % 2 if h else P_BANKS[b], u % 2 * 2 * F:(u % 2 + 1) * 2 * F],
                                             lhsT=hT[:, u, :],
                                             rhs=w1_sb[:, h * 2 * F:(h + 1) * 2 * F], start=True, stop=True)
                    last.then_inc(s["x1_prod"], 1)

            pe.wait_ge(s["we_in"], 16 * len(EA_GROUPS))
            pe.wait_ge(s["p_done"], NCH * 4 + 4)
            pe.wait_ge(s["q_staged"], NCH * 4 + 2)
            w_regs = [pe.alloc_register(f"pe_w{u}") for u in range(UB)]

            def load_windows(first):
                pe.reg_load(w_regs, regs[0:1, bass.ds(first + NC * P, UB)])
                return [pe.snap(r, min_val=0, max_val=(NW - 1) * 2 * F) for r in w_regs]

            def ok(g):
                return not isinstance(g, int) or 0 <= g < NG

            def conv_step(j, slot, m, wins, shift):
                g = j - 1
                if ok(g):
                    pe.wait_ge(s["oh_copied"], g + 3)
                    turn = g // GB if isinstance(g, int) else m - (1 if slot == 0 else 0)
                    pe.wait_ge(s_ea[(slot - 1) % GB], (turn + 1) * 64)
                    pe.wait_ge(s["added"], g + 3)
                    for t in range(G):
                        o = ps_pre[:, (slot - 1) % 2, t, :]
                        te.matmul(o, lhsT=ohT[:, (slot - 1) % 2, t, :],
                                  rhs=pq[:, bass.ds(wins[(slot - shift) * G + t], 2 * F)],
                                  start=True, stop=False)
                        last = te.matmul(o, lhsT=ea_sb[:, (slot - 1) % GB * G + t, :], rhs=we_rows[:, :],
                                         start=False, stop=True)
                    last.then_inc(s["pre_ready"], 1)
                if ok(j):
                    pe.wait_ge(s["oh1"], j + 1)
                    pe.wait_ge(s["oh_copied"], j + 1)
                    for t in range(G):
                        last = te.transpose(ps_ohT[:, slot % 2, t, :], oh[:, slot, t, :], ident[:, :])
                    last.then_inc(s["oh_tr"], 1)
                g = j - 3
                if ok(g):
                    pe.wait_ge(s["msgd"], g + 1 + 1)
                    pe.wait_ge(s["agg_added"], g * G + G)
                    for t in range(G):
                        last = te.matmul(ps_agg[:, (slot - 3) % 2, t, :], lhsT=oh[:, (slot - 3) % GB, t, :],
                                         rhs=mm[:, (slot - 3) % 2, t, :], start=True, stop=True)
                    last.then_inc(s["agg"], 1)

            wins = load_windows(0)
            for j in range(GB):
                conv_step(j, j, 0, wins, 1)
            with pe.Fori(1, NG // GB) as m:
                wins = load_windows(m * UB - G)
                for g in range(GB):
                    conv_step(m * GB + g, g, m, wins, 0)
            wins = load_windows(NS - G)
            for j in range(NG, NG + GB):
                conv_step(j, j % GB, NG // GB, wins, 0)
            pe.wait_ge(s["agg_added"], NS + 8)
            a3 = acc[:, :].rearrange("p (w f) -> p w f", f=FA)
            for w in range(0, NW, 4):
                n = min(4, NW - w)
                last = te.matmul(ps[:, 0, 0:n * F], lhsT=ones[:, :], rhs=a3[:, w:w + n, 0:F],
                                 start=w == 0, stop=w + n == NW)
            last.then_inc(s["bn_sum"], 1)
            for i, w in enumerate(range(0, NW, 4)):
                n = min(4, NW - w)
                pe.wait_ge(s["sq_ready"], i + 1)
                te.matmul(ps[:, 1, 0:n * F], lhsT=mask[:, :] if w + n == NW else ones[:, :],
                          rhs=work[:, 5376 + i % 2 * 512:5376 + i % 2 * 512 + n * F],
                          start=w == 0, stop=w + n == NW).then_inc(s["sq_used"], 1)

        @block.scalar
        def _(act):
            sc = nc.scalar
            act.dma_start(bl2[:, :], every_partition(bl[2, :], F)).then_inc(s["loads"], 16)
            act.dma_start(b1_sb[:, :], every_partition(b1, 2 * F)).then_inc(s["loads"], 16)
            act.dma_start(bn_sb[:, :, :].rearrange("p a f -> p (a f)"), every_partition(bn, 4 * F)).then_inc(s["loads"], 16)
            act.dma_start(blT_sb[:, :], blT).then_inc(s["loads"], 16)
            act.dma_start(w1_sb[:, :], w1).then_inc(s["loads"], 16)
            act.dma_start(we_sb[:, :], we).then_inc(s["loads"], 16)
            half = NW // 2 * P
            xv = x.rearrange("(w p) f -> p w f", p=P)
            xs = x_sb[:, :].rearrange("p (w f) -> p w f", f=F)
            act.dma_start(xs[:, 0:NW // 2, :], xv[:, 0:NW // 2, :]).then_inc(s["loads"], 16)
            act.dma_start(xs[:, NW // 2:NW, :], xv[:, NW // 2:NW, :]).then_inc(s["loads"], 16)
            def first_products(it):
                act.wait_ge(s["products"], (it + 1) * 4 + 1)
                sc.copy(y_staged(it % 2), ps_prod[:, 0:CW, 0:F]).then_inc(s["prod_act"], 2)
                sc.copy(chunk(res, it, F), ps_prod[:, 0:CW, F:2 * F]).then_inc(s["prod_dve"], 2)

            first_products(0)
            with act.Fori(1, NCH) as it:
                act.wait_ge(s["y_free"], it)
                first_products(it)
            act.wait_ge(s["rows_tr"], 1)
            act.wait_ge(s["loads"], LOADS * 16)
            sc.copy(dlo[:, :], ps_tr[:, 0:NC, :].rearrange("p c e -> p (c e)")).then_inc(s["dlo_ready"], 1)
            act.wait_ge(s["srcs_ready"], 1)

            def ea_first_part(n):
                act.wait_ge(s["ea_in"], (n + 1) * 16)
                act.wait_ge(s["ea_free"], n + 1)
                alone(act)
                sc.copy(ea_part[0], ea_chunk(n)).then_inc(s["ea_1"], 1)

            def ea_next_part(n, k):
                act.wait_ge(s[f"ea_r{k}"], n + 1)
                alone(act)
                sc.copy(ea_part[k], ea_chunk(n)).then_inc(s[f"ea_{k + 1}"], 1)

            def sage_indices(layer, a=0, b=NS // UB, first_part=False, other_parts=False):
                with act.Fori(a, b) as it:
                    for half in range(2):
                        at_ = it * UB + half * (UB // 2)
                        act.wait_ge(s["tiles_summed"], layer * NS + at_ + UB // 2)
                        sc.copy(idx[:, half * UB // 2:(half + 1) * UB // 2], srcs[:, bass.ds(at_, UB // 2)])\
                            .then_inc(s["idx_ready"], 1)
                        if other_parts:
                            ea_next_part(it - 1, half + 1)
                    if first_part:
                        ea_first_part(it)

            with act.Fori(0, 2) as layer:
                sage_indices(layer)
                with act.Fori(0, NCH) as it:
                    c = layer * NCH + it
                    act.wait_ge(s["products"], (c + NCH) * 4 + 1)
                    for k, wins in enumerate(QUADS):
                        act.wait_ge(s["h_transposed"], c * 2 + k + 1 + 1)
                        alone(act)
                        sc.activation(hT[:, wins[0]:wins[-1] + 1, :], ps_tr[:, wins[0]:wins[-1] + 1, :], ACT.Relu,
                                      bias=blT_sb[:, bass.ds(layer, 1)]).then_inc(s["h_copied"], 1)
                    act.wait_ge(s["y_free"], c + NCH)
                    for b in (0, 2):
                        act.wait_ge(s["products"], (c + NCH) * 4 + b + 1 + 1)
                        w, n = PAIRS[b][0], len(PAIRS[b])
                        sc.copy(y_staged(it % 2, w, n), ps_prod[:, w:w + n, 0:F])
                        sc.copy(res[:, bass.ds(it * (CW * F) + w * F, n * F)].rearrange("p (u f) -> p u f", f=F),
                                ps_prod[:, w:w + n, F:2 * F]).then_inc(s["prod_act"], 1)
            sage_indices(2, 0, 1, first_part=True)
            sage_indices(2, 1, EA_TURNS, first_part=True, other_parts=True)
            sage_indices(2, EA_TURNS, EA_TURNS + 1, other_parts=True)
            sage_indices(2, EA_TURNS + 1)
            act.preload_act_table_set("natural_log_exp_and_others")

            def inverse_deviation(k, n, ve_, rs_, used):
                act.wait_ge(s["var_" + k], n + 1)
                if not isinstance(n, int) or n > 0:
                    act.wait_ge(s[used[0]], n + used[1])
                sc.activation(rs_[:, :], ve_[:, :], ACT.Ln).then_inc(s["rs_" + k], 1)
                act.wait_ge(s["rs_" + k], n * 2 + 1)
                sc.activation(rs_[:, :], rs_[:, :], ACT.Exp, scale=-0.5).then_inc(s["rs_" + k], 1)

            def apply_norm(out_, in_, rs_, nm_):
                for u in range(CW):
                    last = sc.activation(out_[:, u, :], in_[:, u, :], ACT.Identity, bias=nm_[:, u:u + 1],
                                         scale=rs_[:, u:u + 1])
                return last

            def norm_x1(it):
                inverse_deviation("z", it, ve, rs, ("x1_ready", 0))
                act.wait_ge(s["coef_z"], it + 1)
                act.wait_ge(s["x_kept"], it + 1)
                act.wait_ge(s["x1_tr"], it * 2 + 1)
                apply_norm(x1c, hr, rs, nm).then_inc(s["x1_ready"], 1)

            def copy_q(it, last):
                act.wait_ge(s["x1_prod"], it * 4 + 1)
                for k, wins in enumerate(QUADS):
                    act.wait_ge(s["x1_tr"], it * 2 + k + 1 + 1)
                    sc.copy(hT[:, wins[0]:wins[-1] + 1, :], ps_tr[:, wins[0]:wins[-1] + 1, :]).then_inc(s["x1_copied"], 1)
                act.wait_ge(s["q_free"], it + 1)
                for b, wins in enumerate(PAIRS):
                    n = len(wins)
                    if b == 2 and not last:
                        norm_x1(it + 1)
                    act.wait_ge(s["x1_prod"], it * 4 + b + 1 + 1)
                    sc.copy(q_staged(it % 2, wins[0], n),
                            ps[:, 2 + b % 2, 0:n * 2 * F].rearrange("p (u f) -> p u f", f=2 * F)).then_inc(s["q_staged"], 1)

            norm_x1(0)
            with act.Fori(0, NCH - 1) as it:
                copy_q(it, False)
            copy_q(NCH - 1, True)

            def ok(g):
                return not isinstance(g, int) or 0 <= g < NG

            def indices(g, slot):
                act.wait_ge(s["added"], g + 1)
                sc.copy(idx[:, slot * G:(slot + 1) * G], srcs[:, bass.ds(g * G, G)]).then_inc(s["qi"], 1)

            def conv_step(j, slot):
                g = j - 2
                if ok(g):
                    act.wait_ge(s["added"], g + 5)
                    if not isinstance(g, int) or g >= 1:
                        act.wait_ge(s["spd"], g)
                    log_ = lg[:, slot % 2, :, :]
                    sc.activation(log_, pre[:, slot % 2, :, :], ACT.Abs).then_inc(s["absd"], 1)
                if ok(j - 3):
                    act.wait_ge(s["diffd"], j - 3 + 2)
                    sc.activation(sg, sg, ACT.Exp).then_inc(s["sigd"], 1)
                if ok(g):
                    act.wait_ge(s["absd"], g + 1)
                    sc.activation(log_, log_, ACT.Exp, scale=-1.0).then_inc(s["expd"], 1)
                    act.wait_ge(s["expd"], g + 1)
                    sc.activation(log_, log_, ACT.Ln, bias=1.0).then_inc(s["logd"], 1)
                if ok(j + 2) and ok(j):
                    indices(j + 2, (slot + 2) % GB)
                if ok(j):
                    act.wait_ge(s["oh_tr"], j + 1)
                    act.wait_ge(s["pre_ready"], j + 3)
                    sc.copy(ohT[:, slot % 2, :, :], ps_ohT[:, slot % 2, :, :]).then_inc(s["oh_copied"], 1)

            act.wait_ge(s["q_written"], NCH * 16)
            act.wait_ge(s["x_kept"], NCH + 1)
            indices(0, 0)
            indices(1, 1)
            for j in range(GB):
                conv_step(j, j)
            with act.Fori(1, NG // GB - 1) as m:
                for g in range(GB):
                    conv_step(m * GB + g, g)
            for j in range(NG - GB, NG + GB):
                conv_step(j, j % GB)
            for i, w in enumerate(range(0, NW, 4)):
                n = min(4, NW - w)
                act.wait_ge(s["cen_ready"], i + 1)
                if i >= 2:
                    act.wait_ge(s["sq_used"], i - 1)
                sc.activation(work[:, 5376 + i % 2 * 512:5376 + i % 2 * 512 + n * F], cen[:, w * F:(w + n) * F],
                              ACT.Square).then_inc(s["sq_ready"], 1)
            act.wait_ge(s["bv_var"], 1)
            sc.activation(small[:, 1, :], small[:, 0, :], ACT.Ln).then_inc(s["bv_rs"], 1)
            act.wait_ge(s["bv_rs"], 1)
            sc.activation(small[:, 1, :], small[:, 1, :], ACT.Exp, scale=-0.5).then_inc(s["bv_rs"], 1)

            def last_norms(a, b):
                if a is not None:
                    inverse_deviation("a", a, ve_a, rs_a, ("normed_a", 0))
                if b is not None:
                    inverse_deviation("b", b, ve_b, rs_b, ("o_ready", 1))
                if a is not None:
                    act.wait_ge(s["coef_a"], a + 1)
                    if not isinstance(a, int) or a > 0:
                        act.wait_ge(s["a_used"], a)
                        alone(act)
                    hc = chunk(cen, a, F)
                    apply_norm(tmp, hc, rs_a, nm_a).then_inc(s["normed_a"], 1)
                if b is not None:
                    act.wait_ge(s["coef_b"], b + 1)
                    act.wait_ge(s["o_free"], b + 1)
                    alone(act)
                    apply_norm(hr, tmp2, rs_b, nm_b).then_inc(s["o_ready"], 1)

            last_norms(0, None)
            with act.Fori(1, NCH) as it:
                last_norms(it, it - 1)
            last_norms(None, NCH - 1)

        @block.vector
        def _(dve):
            v = nc.vector
            chain = [0]
            base_chain = [0]

            def link(ins):
                chain[0] += 1
                ins.then_inc(s["dve"], 1)
                dve.wait_ge(s["dve"], base_chain[0] + chain[0])

            def in_loop(i, per_turn, before):
                base_chain[0] = before + i * per_turn
                chain[0] = 0

            S0, S_, AF, BF, NE, NN, ONE, C50, D50, DD, IND, KR, TK, WK, W128, JK = range(16)

            def row(r, a=0, b=NB):
                return sch[:, r, a:b]

            v.memset(zero[:, :], 0.0)
            link(v.memset(sch[:, :, :], 0.0))
            dve.wait_ge(s["dnat"], 16)
            link(v.tensor_copy(d_f, d_nat))
            link(v.tensor_tensor(junk, d_f[:, 1:NT + 1], d_f[:, 0:NT], ALU.subtract))
            link(v.tensor_reduce(sch[:, TK, 0:1], junk, X, ALU.min))
            link(v.tensor_scalar(sch[:, S0, NB:NB + 1], sch[:, TK, 0:1], 0.0, None, ALU.is_lt))
            link(v.tensor_single_scalar(d_nat[:, 0:NT], d_nat[:, 0:NT], 7, ALU.arith_shift_right))
            link(v.tensor_copy(d_win, d_nat[:, 0:NT]))
            for w in range(1, NB):
                ins = v.tensor_scalar(junk.bitcast(bf16)[:, 0:NT], d_win, float(w), None, ALU.is_lt, ALU.add,
                                      accum_out=sch[:, S0, w:w + 1])
                if w < NW:
                    link(ins)
            ins.then_inc(s["cnt"], 1)
            dve.wait_ge(s["S"], 1)
            link(v.tensor_copy(row(S_, 0, NB + 1), ps[:, 6, 0:NB + 1]))
            v.tensor_copy(flag[:, :], sch[:, S_, NB:NB + 1])
            v.tensor_copy(schi[:, 0, 0:NB], row(S_))
            link(v.tensor_scalar(row(AF), row(S_), -1.0, None, ALU.add))
            v.tensor_copy(schi[:, 1, 0:NB], row(AF))
            link(v.memset(row(ONE), 1.0))
            link(v.tensor_single_scalar(schi[:, 2:4, 0:NB], schi[:, 0:2, 0:NB], 7, ALU.arith_shift_right))
            v.tensor_copy(row(AF), schi[:, 2, 0:NB])
            link(v.tensor_copy(row(BF), schi[:, 3, 0:NB]))
            link(v.tensor_tensor(row(NN, 0, NW), row(BF, 1, NB), row(AF, 0, NW), ALU.subtract))
            link(v.tensor_tensor(row(NE, 0, NW), row(S_, 1, NB), row(S_, 0, NW), ALU.is_gt))
            link(v.scalar_tensor_tensor(out=row(NN, 0, NW), in0=row(NN, 0, NW), scalar=1.0, in1=row(NE, 0, NW),
                                        op0=ALU.add, op1=ALU.mult))
            link(v.tensor_tensor_scan(row(C50, 1, NB), row(ONE, 0, NW), row(NN, 0, NW), 0.0, ALU.mult, ALU.add))
            link(v.tensor_tensor(row(D50), row(AF), row(C50), ALU.subtract))
            link(v.tensor_tensor(row(DD, 0, NW), row(D50, 1, NB), row(D50, 0, NW), ALU.subtract))
            dve.wait_ge(s["const"], 9)
            for c in range(NC):
                link(v.tensor_scalar(row(IND, 0, NW), row(C50, 1, NB), kcol[:, c:c + 1], None, ALU.is_le, ALU.add,
                                     accum_out=sch[:, WK, c:c + 1]))
                link(v.tensor_tensor_reduce(out=row(JK, 0, NW), in0=row(IND, 0, NW), in1=row(DD, 0, NW), scale=1.0,
                                            scalar=0.0, op0=ALU.mult, op1=ALU.add, accum_out=sch[:, TK, c:c + 1]))
            link(v.tensor_tensor(sch[:, TK, 0:NC], sch[:, TK, 0:NC], kcol[:, :], ALU.add))
            link(v.tensor_scalar(sch[:, TK, 0:NC], sch[:, TK, 0:NC], float(NT - 1), 0.0, ALU.min, ALU.max))
            v.tensor_copy(tki[:, :], sch[:, TK, 0:NC]).then_inc(s["tki"], 1)
            v.tensor_scalar(sch[:, W128, 0:NC], sch[:, WK, 0:NC], float(P), None, ALU.mult)
            v.tensor_scalar(tabf[:, 0, :], sch[:, WK, 0:NC], float(NW - 1), float(FA), ALU.min, ALU.mult)
            v.tensor_scalar(tabf[:, 1, :], sch[:, WK, 0:NC], float(NW - 1), float(2 * F), ALU.min, ALU.mult)
            link(v.tensor_scalar(tabf[:, 2, :], sch[:, TK, 0:NC], float(P), None, ALU.mult))
            v.tensor_copy(tabi[:, :, :], tabf[:, :, :]).then_inc(s["tab"], 1)
            dve.wait_ge(s["tki"], 1)
            unsorted = dve.value_load(flag[0:1, 0:1], min_val=0, max_val=P)
            link(v.tensor_copy(f_base[:, 0:NB], row(S_)))
            with dve.If(unsorted > 0):
                with dve.Fori(0, NT) as t:
                    dve.wait_ge(s["fl"], (t + 1) * 48)
                    f0 = s["f_done"]
                    v.tensor_single_scalar(fhi[:, :], fd[:, :], 7, ALU.arith_shift_right).then_inc(f0, 1)
                    dve.wait_ge(f0, t * 6 + 1)
                    v.tensor_copy(fcol[:, 0:1], fhi[:, :]).then_inc(f0, 1)
                    dve.wait_ge(f0, t * 6 + 2)
                    v.tensor_scalar(fcol[:, 1:2], fcol[:, 0:1], float(NW), None, ALU.min).then_inc(f0, 1)
                    dve.wait_ge(f0, t * 6 + 3)
                    v.tensor_scalar(f_oh[:, 0:NB], iota[:, 0:NB], fcol[:, 1:2], None, ALU.is_equal)\
                        .then_inc(s["f_onehot"], 1)
                    dve.wait_ge(s["f_rank"], t + 1)
                    v.tensor_tensor(f_tmp[:, 0:NB], ps[:, 6, 0:NB], f_base[:, 0:NB], ALU.add).then_inc(f0, 1)
                    dve.wait_ge(f0, t * 6 + 4)
                    v.tensor_tensor_reduce(out=row(JK), in0=f_tmp[:, 0:NB], in1=f_oh[:, 0:NB], scale=1.0, scalar=0.0,
                                           op0=ALU.mult, op1=ALU.add, accum_out=fcol[:, 2:3]).then_inc(f0, 1)
                    v.tensor_tensor(f_base[:, 0:NB], ps[:, 7, 0:NB], f_base[:, 0:NB], ALU.add).then_inc(f0, 1)
                    dve.wait_ge(f0, t * 6 + 6)
                    v.tensor_copy(fpos[:, :], fcol[:, 2:3]).then_inc(s["f_pos"], 1)
            dve.wait_ge(s["products"], NCH * 4 + 1)
            v.memset(acc[:, :], 0.0).then_inc(s["acc_clear"], 1)
            dve.wait_ge(s["rows"], 2 * NC * 16)
            for c in range(NC):
                v.tensor_scalar(d_rowsf[:, c * P:(c + 1) * P], d_rows[:, c * P:(c + 1) * P],
                                sch[:, W128, c:c + 1], None, ALU.subtract)
            v.tensor_copy(s_rowsf, s_rows).then_inc(s["rowsf"], 1)
            dve.wait_ge(s["rows_tr"], 1)
            v.tensor_copy(srcs[:, :], ps_tr[:, 8:8 + NC, :].rearrange("p c e -> p (c e)")).then_inc(s["srcs_ready"], 1)
            dve.wait_ge(s["dlo_ready"], 1)
            dve.wait_ge(s["tab_back"], 64)
            dve.wait_ge(s["acc_clear"], 1)
            dve.wait_ge(s["loads"], LOADS * 16)
            w_regs = [dve.alloc_register(f"dve_w{u}") for u in range(UB)]
            a3 = acc[:, :].rearrange("p (w f) -> p w f", f=FA)

            def load_windows(first):
                dve.reg_load(w_regs, regs[0:1, bass.ds(first, UB)])
                return [dve.snap(r, min_val=0, max_val=(NW - 1) * FA) for r in w_regs]

            def ea_rest(n, k):
                dve.wait_ge(s[f"ea_{k}"], n + 1)
                alone(dve)
                v.tensor_tensor(ea_chunk(n), ea_chunk(n), ea_part[k - 1], ALU.subtract).then_inc(s[f"ea_r{k}"], 1)

            def sage_adds(layer, a=0, b=NS // UB, split=False):
                with dve.Fori(a, b) as it:
                    wins = load_windows(it * UB)
                    first = layer * NS + it * UB

                    def onehot(u):
                        dve.wait_ge(s["tiles_summed"], first + u + 13)
                        v.tensor_scalar(oh4[:, u % 4, :], iota[:, :], dlo[:, bass.ds(it * UB + u, 1)], None,
                                        ALU.is_equal).then_inc(s["onehots"], 1)

                    onehot(0)
                    onehot(1)
                    for u in range(UB):
                        if u + 2 < UB:
                            onehot(u + 2)
                        dve.wait_ge(s["tiles_summed"], first + u + 17)
                        dve.wait_ge(s["tiles_added"], first + u + 4)
                        a = acc[:, bass.ds(wins[u], FA)]
                        v.tensor_tensor(a, a, ps[:, u % 4, 0:FA], ALU.add).then_inc(s["tiles_added"], 1)
                        if split and u % (UB // 2) == UB // 2 - 1:
                            ea_rest(it, u // (UB // 2) + 1)

            def inverse_counts(layer):
                dve.wait_ge(s["tiles_added"], (layer + 1) * NS + 4)
                link(v.tensor_scalar(cnt[:, :], a3[:, :, F], 1.0, None, ALU.max))
                link(v.reciprocal(inv[:, :], cnt[:, :]))
                alone(dve)

            n_links = chain[0]
            with dve.Fori(0, 2) as layer:
                in_loop(layer, 2, n_links)
                sage_adds(layer)
                inverse_counts(layer)
                dve.wait_ge(s["prod_act"], (layer + 1) * (NCH * 2) + 1)
                dve.wait_ge(s["prod_dve"], (layer + 1) * (NCH * 2) + 1)
                alone(dve)
                def new_h(it):
                    c = layer * NCH + it
                    dve.wait_ge(s["h_transposed"], c * 2 + 1)
                    for u in range(CW):
                        w = it * CW + u
                        v.scalar_tensor_tensor(
                            out=hr[:, u, :], in0=acc[:, bass.ds(w * FA, F)], scalar=inv[:, bass.ds(w, 1)],
                            in1=res[:, bass.ds(w * F, F)], op0=ALU.mult, op1=ALU.add).then_inc(s["h_ready"], 1)
                    dve.wait_ge(s["h_ready"], (c + 1) * CW)
                    v.tensor_copy(acc[:, bass.ds(it * (CW * FA), CW * FA)], zero[:, :].to_broadcast([P, CW * FA]))\
                        .then_inc(s["acc_clear"], 1)

                def copy_products(it):
                    c = layer * NCH + it
                    dve.wait_ge(s["y_free"], c + NCH)
                    for b in (1, 3):
                        dve.wait_ge(s["products"], (c + NCH) * 4 + b + 1 + 1)
                        w, n = PAIRS[b][0], len(PAIRS[b])
                        v.tensor_copy(y_staged(it % 2, w, n), ps_prod[:, w:w + n, 0:F])
                        v.tensor_copy(res[:, bass.ds(it * (CW * F) + w * F, n * F)].rearrange("p (u f) -> p u f", f=F),
                                      ps_prod[:, w:w + n, F:2 * F]).then_inc(s["prod_dve"], 1)

                new_h(0)
                with dve.Fori(1, NCH) as it:
                    new_h(it)
                    copy_products(it - 1)
                copy_products(NCH - 1)
                dve.wait_ge(s["acc_clear"], (layer + 1) * NCH + 1)
            n_links += 4
            in_loop(0, 0, n_links)
            link(v.tensor_tensor(x_sb[:, :].rearrange("p (u f) -> p u f", f=F),
                                 x_sb[:, :].rearrange("p (u f) -> p u f", f=F),
                                 bl2[:, :].unsqueeze(1).to_broadcast([P, NW, F]), ALU.add))
            for k in range(3):
                last = v.tensor_copy(we_part[:, k, :], we_sb[:, :])
                if k < 2:
                    link(last)
                    link(v.tensor_tensor(we_sb[:, :], we_sb[:, :], we_part[:, k, :], ALU.subtract))
            last.then_inc(s["we_split"], 1)
            sage_adds(2, 0, EA_TURNS, split=True)
            sage_adds(2, EA_TURNS)
            inverse_counts(2)
            dve.wait_ge(s["prod_act"], 3 * NCH * 2 + 1)
            dve.wait_ge(s["prod_dve"], 3 * NCH * 2 + 1)
            n_links += 7

            def statistics(k, src_, st, mv_, ve_):
                for u in range(CW):
                    last = v.bn_stats(st[:, u, :], src_[:, u, :])
                link(last)
                alone(dve)
                for u in range(CW):
                    last = v.bn_aggr(mv_[:, u, :], st[:, u, :])
                link(last)
                v.tensor_scalar(ve_[:, :], mv_[:, :, 1], EPS, None, ALU.add).then_inc(s["var_" + k], 1)

            def coefficients(k, n, mv_, ve_, rs_, nm_):
                dve.wait_ge(s["var_" + k], n + 1)
                dve.wait_ge(s["rs_" + k], (n + 1) * 2)
                newton(rs_[:, :], ve_[:, :], rt[:, :])
                v.scalar_tensor_tensor(out=nm_[:, :], in0=mv_[:, :, 0], scalar=-1.0, in1=rs_[:, :], op0=ALU.mult,
                                       op1=ALU.mult).then_inc(s["coef_" + k], 1)

            def newton(y, var_, t):
                link(v.tensor_tensor(t, y, y, ALU.mult))
                link(v.tensor_tensor(t, t, var_, ALU.mult))
                link(v.tensor_scalar(t, t, -0.5, 1.5, ALU.mult, ALU.add))
                link(v.tensor_tensor(y, y, t, ALU.mult))

            per = 8
            def new_x1(it):
                in_loop(it, per, n_links)
                if not isinstance(it, int) or it > 1:
                    add_b1(it - 2)
                if not isinstance(it, int) or it > 0:
                    dve.wait_ge(s["x1_ready"], it)
                for u in range(CW):
                    w = it * CW + u
                    last = v.scalar_tensor_tensor(
                        out=hr[:, u, :], in0=acc[:, bass.ds(w * FA, F)], scalar=inv[:, bass.ds(w, 1)],
                        in1=res[:, bass.ds(w * F, F)], op0=ALU.mult, op1=ALU.add)
                link(last)
                link(v.tensor_tensor(hr, hr, chunk(x_sb, it, F), ALU.add))
                statistics("z", hr, st6, mv, ve)
                coefficients("z", it, mv, ve, rs, nm)
                v.tensor_copy(acc[:, bass.ds(it * (CW * FA), CW * FA)], zero[:, :].to_broadcast([P, CW * FA]))\
                    .then_inc(s["acc_clear"], 1)
                assert chain[0] == per, chain[0]

            def add_b1(it):
                for b, wins in enumerate(PAIRS):
                    n = len(wins)
                    dve.wait_ge(s["x1_prod"], it * 4 + b + 1 + 1)
                    v.tensor_tensor(
                        pq[:, bass.ds(it * (CW * 2 * F) + wins[0] * 2 * F, n * 2 * F)].rearrange("p (u f) -> p u f", u=n),
                        ps[:, P_BANKS[b], 0:n * 2 * F].rearrange("p (u f) -> p u f", u=n),
                        b1_sb[:, :].unsqueeze(1).to_broadcast([P, n, 2 * F]), ALU.add).then_inc(s["p_done"], 1)

            dve.wait_ge(s["ea_free"], EA_TURNS + 1)
            new_x1(0)
            new_x1(1)
            with dve.Fori(2, NCH) as it:
                new_x1(it)
            add_b1(NCH - 2)
            add_b1(NCH - 1)
            n_links += per * NCH
            dve.wait_ge(s["acc_clear"], 3 * NCH + 1)
            dve.wait_ge(s["x_kept"], NCH + 1)
            dve.wait_ge(s["q_written"], NCH * 16)

            def ok(g):
                return not isinstance(g, int) or 0 <= g < NG

            def conv_step(j, slot, m, wins):

                def add_sum(t):
                    g = j - 4
                    if ok(g):
                        if t == 0:
                            dve.wait_ge(s["agg"], g + 5)
                        dve.wait_ge(s["agg_added"], g * G + t + 8)
                        a = acc[:, bass.ds(wins[slot * G + t], F)]
                        v.tensor_tensor(a, a, ps_agg[:, slot % 2, t, :], ALU.add).then_inc(s["agg_added"], 1)

                g = j - 2
                if ok(g):
                    dve.wait_ge(s["pre_ready"], g + 5)
                    turn = g // GB if isinstance(g, int) else m - (1 if slot < 2 else 0)
                    dve.wait_ge(s_qg[(slot - 2) % GB], (turn + 1) * 64)
                    if not isinstance(g, int) or g >= 1:
                        dve.wait_ge(s["spd"], g)
                        dve.wait_ge(s["diffd"], g)
                    v.tensor_tensor(pre[:, slot % 2, :, :], ps_pre[:, slot % 2, :, :], qg[:, (slot - 2) % GB, :, :],
                                    ALU.add).then_inc(s["added"], 1)
                add_sum(0)
                g = j - 3
                pre_, log_ = pre[:, (slot - 3) % 2, :, :], lg[:, (slot - 3) % 2, :, :]
                if ok(g):
                    dve.wait_ge(s["logd"], g + 1)
                    dve.wait_ge(s["msgd"], g + 1)
                    v.scalar_tensor_tensor(out=sg, in0=pre_[:, :, 0:F], scalar=0.0, in1=log_[:, :, 0:F],
                                           op0=ALU.min, op1=ALU.subtract).then_inc(s["diffd"], 1)
                add_sum(1)
                if ok(g):
                    v.scalar_tensor_tensor(out=sp_, in0=pre_[:, :, F:2 * F], scalar=0.0, in1=log_[:, :, F:2 * F],
                                           op0=ALU.max, op1=ALU.add).then_inc(s["spd"], 1)
                add_sum(2)
                if ok(j):
                    dve.wait_ge(s["agg"], j + 1)
                    v.tensor_tensor(oh[:, slot, :, :], iota[:, :].unsqueeze(1).to_broadcast([P, G, P]),
                                    dlo[:, bass.ds(j * G, G)].unsqueeze(2).to_broadcast([P, G, P]), ALU.is_equal)\
                        .then_inc(s["oh1"], 1)
                add_sum(3)
                if ok(g):
                    dve.wait_ge(s["sigd"], g + 1)
                    dve.wait_ge(s["spd"], g + 2)
                    dve.wait_ge(s["agg"], g + 3)
                    v.tensor_tensor(mm[:, (slot - 3) % 2, :, :], sg, sp_, ALU.mult).then_inc(s["msgd"], 1)

            for j in range(GB):
                conv_step(j, j, 0, None)
            with dve.Fori(1, NG // GB) as m:
                wins = load_windows(m * UB - UB)
                for g in range(GB):
                    conv_step(m * GB + g, g, m, wins)
            wins = load_windows(NS - UB)
            for j in range(NG, NG + GB):
                conv_step(j, j % GB, NG // GB, wins)
            in_loop(0, 0, n_links)
            dve.wait_ge(s["bn_sum"], 1)
            link(v.tensor_reduce(small[:, 2, :], ps[:, 0, :].rearrange("p (a f) -> p f a", f=F), X, ALU.add))
            link(v.tensor_scalar(mean[:, :], small[:, 2, :], 1.0 / N, None, ALU.mult))
            for w in range(0, NW, 4):
                n = min(4, NW - w)
                v.tensor_tensor(cen[:, w * F:(w + n) * F].rearrange("p (u f) -> p u f", f=F), a3[:, w:w + n, 0:F],
                                mean[:, :].unsqueeze(1).to_broadcast([P, n, F]), ALU.subtract).then_inc(s["cen_ready"], 1)
            NQ = -(-NW // 4)
            dve.wait_ge(s["sq_used"], NQ)
            link(v.tensor_reduce(small[:, 3, :], ps[:, 1, :].rearrange("p (a f) -> p f a", f=F), X, ALU.add))
            v.tensor_scalar(small[:, 0, :], small[:, 3, :], 1.0 / N, EPS, ALU.mult, ALU.add).then_inc(s["bv_var"], 1)
            dve.wait_ge(s["bv_var"], 1)
            dve.wait_ge(s["bv_rs"], 2)
            newton(small[:, 1, :], small[:, 0, :], small[:, 2, :])
            v.tensor_tensor(bscale[:, :], small[:, 1, :], bn_sb[:, 0, :], ALU.mult).then_inc(s["bv_rs"], 1)
            n_links += chain[0]
            def last_norms(a, b):
                if a is not None:
                    dve.wait_ge(s["h_scaled"], a * 4 + 3)
                    alone(dve)
                    statistics("a", chunk(cen, a, F), st_a, mv_a, ve_a)
                if b is not None:
                    dve.wait_ge(s["normed_a"], b + 1)
                    link(v.tensor_tensor(tmp, tmp, bn_sb[:, 2, :].unsqueeze(1).to_broadcast([P, CW, F]), ALU.mult))
                    link(v.tensor_tensor(tmp, tmp, bn_sb[:, 3, :].unsqueeze(1).to_broadcast([P, CW, F]), ALU.add))
                    dve.wait_ge(s["o_ready"], b + 1)
                    dve.wait_ge(s["h_scaled"], b * 4 + 4)
                    v.scalar_tensor_tensor(out=tmp2, in0=tmp, scalar=0.0, in1=chunk(x_sb, b, F),
                                           op0=ALU.max, op1=ALU.add).then_inc(s["a_used"], 1)
                    dve.wait_ge(s["a_used"], b + 1)
                    statistics("b", tmp2, st_b, mv_b, ve_b)
                if a is not None:
                    coefficients("a", a, mv_a, ve_a, rs_a, nm_a)
                if b is not None:
                    coefficients("b", b, mv_b, ve_b, rs_b, nm_b)

            in_loop(0, 0, n_links)
            last_norms(0, None)
            n_links += chain[0]
            per = 14
            with dve.Fori(1, NCH) as it:
                in_loop(it, per, n_links - per)
                last_norms(it, it - 1)
                assert chain[0] == per, chain[0]
            in_loop(0, 0, n_links + (NCH - 1) * per)
            last_norms(None, NCH - 1)


_INS = ["x", "xT", "src", "dst", "ea", "eaT", "w0", "bl", "blT", "w1", "we", "b1", "bn"]


def kernel(**inputs):
    import numpy as np
    import concourse.bacc as bacc
    from concourse.bass_utils import run_bass_kernel_spmd

    a = {k: np.asarray(v) for k, v in inputs.items()}
    f = np.float32

    def padded(v, n, fill=0):
        return np.concatenate([v, np.full((n - v.shape[0],) + v.shape[1:], fill, v.dtype)])

    x = padded(a["x"], NP)
    ea = padded(a["edge_attr_16"], EP)
    wf, ws = a["L1_gnn_Wf"].T, a["L1_gnn_Ws"].T
    arrays = {
        "x": x, "xT": x.T,
        "src": padded(a["src"], EP), "dst": padded(a["dst"], EP + P, PAD),
        "ea": ea, "eaT": ea.T,
        "w0": np.concatenate([a["L0_gnn_Wl"], a["L0_gnn_Wr"]], axis=2),
        "bl": a["L0_gnn_bl"], "blT": a["L0_gnn_bl"].T,
        "w1": np.concatenate([wf[0:F], ws[0:F], wf[F:2 * F], ws[F:2 * F]], axis=1),
        "we": np.concatenate([wf[2 * F:], ws[2 * F:]], axis=1),
        "b1": np.concatenate([a["L1_gnn_bf"], a["L1_gnn_bs"]]),
        "bn": np.concatenate([a["L1_gnn_bn_gamma"], a["L1_gnn_bn_beta"], a["L1_gnn_ln_gamma"], a["L1_gnn_ln_beta"]]),
    }
    nc = bacc.Bacc("TRN2", target_bir_lowering=False, num_devices=1)
    ins, args = {}, []
    for name in _INS:
        v = np.ascontiguousarray(arrays[name])
        ins[f"in_{name}"] = v
        args.append(nc.dram_tensor(f"in_{name}", v.shape, mybir.dt.from_np(v.dtype), kind="ExternalInput").ap())
    out = nc.dram_tensor("out", (N, F), mybir.dt.from_np(np.dtype(f)), kind="ExternalOutput").ap()
    build_gnn(nc, *args, out)
    r = run_bass_kernel_spmd(nc, [ins], core_ids=[0])
    return r.results[0]["out"]
```
